# Optimizing a Trainium2 kernel written in Bass

```python
import numpy as np
import jax
import jax.numpy as jnp

def _softmax(x, axis=-1):
    return jax.nn.softmax(x, axis=axis)

def _gelu(x):
    return jax.nn.gelu(x, approximate=True)

def _silu(x):
    return jax.nn.silu(x)

def _sigmoid(x):
    return jax.nn.sigmoid(x)

def _layernorm(x, axis=-1, eps=1e-05):
    m = jnp.mean(x, axis=axis, keepdims=True)
    v = jnp.var(x, axis=axis, keepdims=True)
    return (x - m) / jnp.sqrt(v + eps)

def _scatter_add(tgt, idx, src, axis=0):
    return tgt.at[idx].add(src)

def _segment_sum(src, seg, n):
    return jax.ops.segment_sum(src, seg, n)
kernel_name = 'mk_gps_d1_gnn_r8_ab60ba'

def setup_inputs(seed: int=0):
    np.random.seed(seed)
    _w = jnp.asarray

    def _rec_inputs():
        import jax
        import jax.numpy as jnp
        _gk = jax.random.key(seed)
        x = -0.0002117 + 1 * jax.random.normal(jax.random.fold_in(_gk, 1), (6250, 256), jnp.float32)
        src = jax.random.randint(jax.random.fold_in(_gk, 2), (200000,), 0, 6250, jnp.int32)
        dst = jax.random.randint(jax.random.fold_in(_gk, 3), (200000,), 0, 6250, jnp.int32)
        _o = jnp.argsort(dst, stable=True)
        src = src[_o]
        dst = dst[_o]
        edge_weight = jax.random.uniform(jax.random.fold_in(_gk, 12), (200000,), jnp.float32, 0.0, 1)
        return (x, src, dst, edge_weight)
    x, src, dst, edge_weight = _rec_inputs()

    def _L0_gnn_setup():
        import jax, jax.numpy as jnp
        import numpy as np
        N_NODES = 12500
        N_EDGES = 400000
        D = 256

        def _graph_conv(x, W, edge_src, edge_dst, edge_weight, n_nodes):
            support = x @ W
            msg = support[edge_src] * edge_weight[:, None]
            return jax.ops.segment_sum(msg, edge_dst, num_segments=n_nodes)
        key = jax.random.key(seed)
        k1, k2, k3, k4, k5, k6 = jax.random.split(key, 6)
        scale = 1.0 / np.sqrt(D)
        return {'features': jax.random.normal(k1, (N_NODES, D), dtype=jnp.float32), 'edge_weight': jax.random.uniform(k2, (N_EDGES,), dtype=jnp.float32), 'W1': jax.random.normal(k3, (D, D), dtype=jnp.float32) * scale, 'W2': jax.random.normal(k4, (D, D), dtype=jnp.float32) * scale, 'edge_src': jax.random.randint(k5, (N_EDGES,), 0, N_NODES, dtype=jnp.int32), 'edge_dst': jax.random.randint(k6, (N_EDGES,), 0, N_NODES, dtype=jnp.int32)}
    _L0_gnn_all = _L0_gnn_setup()
    _L0_gnn_in = {k: v for k, v in _L0_gnn_all.items() if k in ('W1', 'W2')}
    del _L0_gnn_all

    def _L0_mix_setup():
        import jax, jax.numpy as jnp
        import numpy as np
        import math
        EMBED = 256
        HEADS = 4
        HEAD_DIM = EMBED // HEADS
        OUT_DIM = 256
        LN_EPS = 1e-05

        def _qkv_init(key):
            spread = math.sqrt(3.0 / EMBED)
            gain, delta = (0.01, 0.01)
            w = jax.random.uniform(key, (EMBED, EMBED), minval=-spread, maxval=spread) * gain
            return w + delta * jnp.eye(EMBED, dtype=w.dtype)

        def _layer_norm(x, g, b):
            mu = jnp.mean(x, axis=-1, keepdims=True)
            var = jnp.mean(jnp.square(x - mu), axis=-1, keepdims=True)
            return (x - mu) * jax.lax.rsqrt(var + LN_EPS) * g + b

        def _split_heads(x, B, S):
            return x.reshape(B, S, HEADS, HEAD_DIM).transpose(0, 2, 1, 3)
        key = jax.random.key(seed)
        ks = jax.random.split(key, 6)
        seq = jax.random.normal(ks[0], (4, 1024, EMBED), dtype=jnp.float32)
        wq = _qkv_init(ks[1])
        wk = _qkv_init(ks[2])
        wv = _qkv_init(ks[3])
        bound = 1.0 / math.sqrt(EMBED)
        wo = jax.random.uniform(ks[4], (OUT_DIM, EMBED), minval=-bound, maxval=bound)
        bo = jax.random.uniform(ks[5], (OUT_DIM,), minval=-bound, maxval=bound)
        ln_k_g = jnp.ones((HEAD_DIM,), jnp.float32)
        ln_k_b = jnp.zeros((HEAD_DIM,), jnp.float32)
        ln_v_g = jnp.ones((HEAD_DIM,), jnp.float32)
        ln_v_b = jnp.zeros((HEAD_DIM,), jnp.float32)
        return {'seq': seq, 'wq': wq, 'wk': wk, 'wv': wv, 'wo': wo, 'bo': bo, 'ln_k_g': ln_k_g, 'ln_k_b': ln_k_b, 'ln_v_g': ln_v_g, 'ln_v_b': ln_v_b}
    _L0_mix_all = _L0_mix_setup()
    _L0_mix_in = {k: v for k, v in _L0_mix_all.items() if k in ('wq', 'wk', 'wv', 'wo', 'bo', 'ln_k_g', 'ln_k_b', 'ln_v_g', 'ln_v_b')}
    del _L0_mix_all

    def _L0_ffn_setup():
        import jax, jax.numpy as jnp
        import numpy as np
        B, S, H, F, E, K = (8, 512, 256, 512, 16, 2)
        EPS = 1e-05
        key = jax.random.key(seed)
        ks = jax.random.split(key, 9)
        sc = 0.02
        return {'x': jax.random.normal(ks[0], (B, S, H), dtype=jnp.float32), 'gate_w': jax.random.normal(ks[1], (H, E), dtype=jnp.float32) * sc, 'gate_b': jnp.zeros((E,), dtype=jnp.float32), 'w1': jax.random.normal(ks[2], (E, H, F), dtype=jnp.float32) * sc, 'b1': jnp.zeros((E, F), dtype=jnp.float32), 'w2': jax.random.normal(ks[3], (E, F, H), dtype=jnp.float32) * sc, 'b2': jnp.zeros((E, H), dtype=jnp.float32), 'gamma': jnp.ones((H,), dtype=jnp.float32), 'beta': jnp.zeros((H,), dtype=jnp.float32)}
    _L0_ffn_all = _L0_ffn_setup()
    _L0_ffn_in = {k: v for k, v in _L0_ffn_all.items() if k in ('gate_w', 'gate_b', 'w1', 'b1', 'w2', 'b2', 'gamma', 'beta')}
    del _L0_ffn_all
    return {'x': x, 'src': src, 'dst': dst, 'edge_weight': edge_weight, 'L0_gnn_W1': _L0_gnn_in['W1'], 'L0_gnn_W2': _L0_gnn_in['W2'], 'L0_mix_wq': _L0_mix_in['wq'], 'L0_mix_wk': _L0_mix_in['wk'], 'L0_mix_wv': _L0_mix_in['wv'], 'L0_mix_wo': _L0_mix_in['wo'], 'L0_mix_bo': _L0_mix_in['bo'], 'L0_mix_ln_k_g': _L0_mix_in['ln_k_g'], 'L0_mix_ln_k_b': _L0_mix_in['ln_k_b'], 'L0_mix_ln_v_g': _L0_mix_in['ln_v_g'], 'L0_mix_ln_v_b': _L0_mix_in['ln_v_b'], 'L0_ffn_gate_w': _L0_ffn_in['gate_w'], 'L0_ffn_gate_b': _L0_ffn_in['gate_b'], 'L0_ffn_w1': _L0_ffn_in['w1'], 'L0_ffn_b1': _L0_ffn_in['b1'], 'L0_ffn_w2': _L0_ffn_in['w2'], 'L0_ffn_b2': _L0_ffn_in['b2'], 'L0_ffn_gamma': _L0_ffn_in['gamma'], 'L0_ffn_beta': _L0_ffn_in['beta']}

def reference(x, src, dst, edge_weight, L0_gnn_W1, L0_gnn_W2, L0_mix_wq, L0_mix_wk, L0_mix_wv, L0_mix_wo, L0_mix_bo, L0_mix_ln_k_g, L0_mix_ln_k_b, L0_mix_ln_v_g, L0_mix_ln_v_b, L0_ffn_gate_w, L0_ffn_gate_b, L0_ffn_w1, L0_ffn_b1, L0_ffn_w2, L0_ffn_b2, L0_ffn_gamma, L0_ffn_beta):
    import jax
    import jax.numpy as jnp

    def _L0_gnn_ref(features, edge_weight, W1, W2, edge_src, edge_dst):
        import jax, jax.numpy as jnp
        import numpy as np
        N_NODES = 12500
        N_EDGES = 400000
        D = 256

        def _graph_conv(x, W, edge_src, edge_dst, edge_weight, n_nodes):
            support = x @ W
            msg = support[edge_src] * edge_weight[:, None]
            return jax.ops.segment_sum(msg, edge_dst, num_segments=n_nodes)
        n = features.shape[0]
        h = _graph_conv(features, W1, edge_src, edge_dst, edge_weight, n)
        out = _graph_conv(h, W2, edge_src, edge_dst, edge_weight, n)
        return out

    def _L0_mix_ref(seq, wq, wk, wv, wo, bo, ln_k_g, ln_k_b, ln_v_g, ln_v_b):
        import jax, jax.numpy as jnp
        import numpy as np
        import math
        EMBED = 256
        HEADS = 4
        HEAD_DIM = EMBED // HEADS
        OUT_DIM = 256
        LN_EPS = 1e-05

        def _qkv_init(key):
            spread = math.sqrt(3.0 / EMBED)
            gain, delta = (0.01, 0.01)
            w = jax.random.uniform(key, (EMBED, EMBED), minval=-spread, maxval=spread) * gain
            return w + delta * jnp.eye(EMBED, dtype=w.dtype)

        def _layer_norm(x, g, b):
            mu = jnp.mean(x, axis=-1, keepdims=True)
            var = jnp.mean(jnp.square(x - mu), axis=-1, keepdims=True)
            return (x - mu) * jax.lax.rsqrt(var + LN_EPS) * g + b

        def _split_heads(x, B, S):
            return x.reshape(B, S, HEADS, HEAD_DIM).transpose(0, 2, 1, 3)
        B, S, _ = seq.shape
        q = _split_heads(seq @ wq.T, B, S)
        k = _split_heads(seq @ wk.T, B, S)
        v = _split_heads(seq @ wv.T, B, S)
        k = _layer_norm(k, ln_k_g, ln_k_b)
        v = _layer_norm(v, ln_v_g, ln_v_b)
        kv = jnp.einsum('bhsd,bhse->bhde', k, v) / S
        ga = jnp.einsum('bhsd,bhde->bhse', q, kv)
        ga = ga.transpose(0, 2, 1, 3).reshape(B, S, EMBED)
        return ga @ wo.T + bo

    def _L0_ffn_ref(x, gate_w, gate_b, w1, b1, w2, b2, gamma, beta):
        import jax, jax.numpy as jnp
        import numpy as np
        B, S, H, F, E, K = (8, 512, 256, 512, 16, 2)
        EPS = 1e-05
        gate_logits = x @ gate_w + gate_b
        topk_vals, topk_idx = jax.lax.top_k(gate_logits, K)
        topk_w = jax.nn.softmax(topk_vals, axis=-1)
        h = jax.nn.relu(jnp.einsum('bsh,ehf->bsef', x, w1) + b1)
        expert_out = jnp.einsum('bsef,efh->bseh', h, w2) + b2
        sel = jnp.take_along_axis(expert_out, topk_idx[:, :, :, None], axis=2)
        moe = jnp.sum(topk_w[..., None] * sel, axis=2)
        y = x + moe
        mu = jnp.mean(y, axis=-1, keepdims=True)
        var = jnp.var(y, axis=-1, keepdims=True)
        return (y - mu) / jnp.sqrt(var + EPS) * gamma + beta
    xn = _layernorm(x, axis=-1)
    x = x + _L0_gnn_ref(xn, edge_weight, L0_gnn_W1, L0_gnn_W2, src, dst) + _L0_mix_ref(xn[None], L0_mix_wq, L0_mix_wk, L0_mix_wv, L0_mix_wo, L0_mix_bo, L0_mix_ln_k_g, L0_mix_ln_k_b, L0_mix_ln_v_g, L0_mix_ln_v_b)[0]
    x = x + _L0_ffn_ref(_layernorm(x, axis=-1)[None], L0_ffn_gate_w, L0_ffn_gate_b, L0_ffn_w1, L0_ffn_b1, L0_ffn_w2, L0_ffn_b2, L0_ffn_gamma, L0_ffn_beta)[0]
    return x

_drawn_inputs = setup_inputs


def setup_inputs(seed=0):
    import zlib

    import numpy as np

    out = dict(_drawn_inputs(seed))
    spreads = {'L0_mix_ln_k_g': (1.0, 0.6),
     'L0_mix_ln_k_b': (0.0, 0.8),
     'L0_mix_ln_v_g': (1.0, 0.6),
     'L0_mix_ln_v_b': (0.0, 0.8),
     'L0_ffn_gate_b': (0.0, 0.8),
     'L0_ffn_b1': (0.0, 0.8),
     'L0_ffn_b2': (0.0, 2.0),
     'L0_ffn_gamma': (1.0, 0.6),
     'L0_ffn_beta': (0.0, 0.8)}
    factors = {'L0_mix_wq': 8.0,
     'L0_mix_wk': 8.0,
     'L0_mix_wv': 8.0,
     'L0_mix_wo': 8.0,
     'L0_mix_bo': 8.0,
     'L0_ffn_gate_w': 7.064,
     'L0_ffn_w1': 8.0,
     'L0_ffn_w2': 8.0}
    for name, (base, spread) in spreads.items():
        noise = np.random.default_rng([zlib.crc32(name.encode()), seed]).standard_normal(out[name].shape)
        drawn = base * np.exp(spread * noise) if base else spread * noise
        out[name] = jnp.asarray(drawn.astype(out[name].dtype))
    for name, factor in factors.items():
        out[name] = (out[name] * factor).astype(out[name].dtype)
    return out
```

```python
from contextlib import ExitStack

import concourse.bass as bass
from concourse import mybir

F32 = mybir.dt.float32
I32 = mybir.dt.int32
U32 = mybir.dt.uint32
ALU = mybir.AluOpType
ACT = mybir.ActivationFunctionType
AX = mybir.AxisListType

P = 128
N = 6250
D = 256
E = 200000
T = -(-N // P)
NP = T * P
HD = 64
H2 = 2 * D // HD
CG = 8
GB = 4
NG = -(-E // (P * CG * GB)) * GB
NCH = NG * CG
EP = NCH * P
NI = NG // GB
X = 16
FF = 512
ST = (2 * NP) // P + X - 1
SLOTS = ST * P
EPS = 1e-5
STEPS = 2 * NG * T
CT = 7
NC = T // CT
assert NC * CT == T
assert NI == T and T % 2 == 1 and ST % 2 == 1
DG = NG // 2


class Links:

    def __init__(self, eng, sem):
        self.eng, self.sem, self.at, self.n = eng, sem, 0, 0

    def link(self, ins):
        ins.then_inc(self.sem, 1)
        self.n += 1
        self.eng.wait_ge(self.sem, self.at + self.n)

    def turn(self, i, per):
        self.at = self.base + i * per
        self.n = 0

    def enter(self):
        self.base = self.at + self.n

    def leave(self, turns, per):
        assert self.n == per, self.n
        self.at, self.n = self.base + turns * per, 0


def in_pairs(eng, n, tile):
    for b in range(2):
        tile(b, b, 0)
    with eng.Fori(1, n // 2) as j:
        for b in range(2):
            tile(j * 2 + b, b, j)
    tile(n - 1, 0, n // 2)


def wait_from(eng, sem, value):
    if not isinstance(value, int) or value > 0:
        eng.wait_ge(sem, value)


def gps_layer(nc, x, src_t, dst_t, dst_g, wt_t, w1t, gw2, wq, wkv_t, wo_t, bo, kv_g, kv_b,
              gate_w, gate_b, w1, b1_t, w2, b2, gamma, beta, out):
    with ExitStack() as ctx:
        def sb(name, shape, dt=F32):
            return ctx.enter_context(nc.sbuf_tensor(name, shape, dt))

        def sem(name):
            return ctx.enter_context(nc.semaphore(name))

        def dram(name, shape, dt=F32):
            return nc.dram_tensor(name, shape, dt, kind="Internal").ap()

        bank = [ctx.enter_context(nc.psum_tensor(f"bank{n}", [P, 512], F32)) for n in range(8)]

        xn_d = dram("xn_d", [NP, D])
        h1_d = dram("h1_d", [NP, D])
        base_d = dram("base_d", [NP, D])
        x1_d = dram("x1_d", [NP, D])
        y_d = dram("y_d", [NP, D])
        sched_d = dram("sched_d", [NG, 2], I32)
        ys_d = dram("ys_d", [SLOTS, D])
        eo_d = dram("eo_d", [SLOTS, D])

        srcs = sb("srcs", [P, NCH], I32)
        dsti = sb("dsti", [P, NCH], I32)
        dstf = sb("dstf", [P, NCH])
        wts = sb("wts", [P, NCH])
        dgr = sb("dgr", [DG, 2, P * CG], I32)
        mnmx = sb("mnmx", [DG, 2, 2], I32)
        tiles = sb("tiles", [DG, 2, 2], I32)
        trow = sb("trow", [1, NG, 2], I32)
        cnt = sb("cnt", [1, NG])
        one_row = sb("one_row", [1, NG])
        cum = sb("cum", [1, NG])
        tab = sb("tab", [1, 2 * NG, 3], I32)
        iota_n = sb("iota_n", [P, NP])
        ident = sb("ident", [P, P])
        tri = sb("tri", [P, P])
        ones = sb("ones", [P, P])
        zeros = sb("zeros", [P, P])
        wkv = sb("wkv", [P, 2, 2 * D])
        hsum = sb("hsum", [P, 2 * H2])
        w1t_s = sb("w1t_s", [P, 2, D])
        gw2_s = sb("gw2_s", [P, 2, D])
        wq_s = sb("wq_s", [P, 2, D])
        wo_s = sb("wo_s", [P, 2, D])
        w12 = sb("w12", [P, 2, D])
        kvT = sb("kvT", [P, 2, P])
        t1 = sb("t1", [P, 2, D])
        mixm = sb("mixm", [P, 2, D])
        kvg = sb("kvg", [P, 2 * D])
        kvb = sb("kvb", [P, 2 * D])
        bo_s = sb("bo_s", [P, D])
        gam = sb("gam", [P, D])
        bet = sb("bet", [P, D])
        gw = sb("gw", [P, 2, X])
        gb = sb("gb", [P, X])

        acc = sb("acc", [P, T * D])
        gath = [sb(f"gath{b}", [P, CG, D]) for b in range(GB)]
        gidx = [sb(f"gidx{b}", [P, CG], I32) for b in range(GB)]
        hot = [sb(f"hot{k}", [P, P]) for k in range(CG)]
        scr = sb("scr", [P, 8])
        hot2 = [sb(f"osum{b}", [P, D])[:] for b in range(2)]

        xin = [sb(f"xin{b}", [P, D]) for b in range(2)]
        xno = [sb(f"xno{b}", [P, D]) for b in range(2)]
        xT = [sb(f"xT{b}", [P, 2, P]) for b in range(2)]
        yT = [sb(f"yT{b}", [P, 2, P]) for b in range(2)]
        res = [sb(f"res{b}", [P, D]) for b in range(2)]
        sq = sb("sq", [P, 2 * D])
        kvn = sb("kvn", [P, 2 * D])
        r8 = sb("r8", [P, 2, H2])
        st6 = sb("st6", [P, 6])
        mv = sb("mv", [P, 2])
        mva = sb("mva", [P, T, 2])
        sda = sb("sda", [P, T])
        rsa = sb("rsa", [P, T])

        def whole(b):
            return gath[b][:, :, :].rearrange("p c d -> p (c d)")
        we1 = [whole(b)[:, 0:2 * FF].rearrange("p (a f) -> p a f", a=2) for b in range(2)]
        we2 = [whole(b)[:, 2 * FF:2 * FF + 4 * D].rearrange("p (a f) -> p a f", a=4) for b in range(2)]
        hT = [whole(2 + b)[:, 0:512].rearrange("p (a f) -> p a f", a=4) for b in range(2)]
        eo = [whole(2 + b)[:, 512:512 + D] for b in range(2)]
        be2 = [whole(2 + b)[:, 1024:1024 + D] for b in range(2)]
        be1 = [sb(f"be1{b}", [P, 4]) for b in range(2)]
        yb = [whole(b)[:, 0:D] for b in range(4)]
        pidx = [sb(f"pidx{b}", [P, 2], I32) for b in range(2)]

        n_r = T * X

        def rt(n, m=n_r):
            return acc[:, n * n_r:n * n_r + m]
        zero_d = whole(3)[:, 0:8 * D]

        lg = sb("lg", [P, n_r])
        mx = [sb(f"mx{k}", [P, T]) for k in range(2)]
        ix = [sb(f"ix{k}", [P, T]) for k in range(2)]
        pw = [sb(f"pw{k}", [P, T]) for k in range(2)]
        pos = sb("pos", [P, T, 2], I32)
        posf = sb("posf", [P, T, 2])
        iota_x = sb("iota_x", [P, X])
        nt_i = sb("nt_i", [P, X], I32)
        nt_f = sb("nt_f", [P, 3, X])
        eid = sb("eid", [1, ST], I32)

        s_wt = sem("s_wt"); s_pool = sem("s_pool"); s_pc = sem("s_pc"); s_dve = sem("s_dve")
        s_x = [sem(f"s_x{c}") for c in range(NC)]; s_xv = sem("s_xv"); s_xs = sem("s_xs")
        s_xn = sem("s_xn"); s_xst = sem("s_xst"); s_m_var = sem("s_m_var"); s_m_sd = sem("s_m_sd")
        s_sch = sem("s_sch"); s_sch_st = sem("s_sch_st"); s_sch_ld = sem("s_sch_ld"); s_tab = sem("s_tab")
        s_gx = sem("s_gx"); s_g = [sem(f"s_g{b}") for b in range(GB)]; s_gdone = sem("s_gdone")
        s_oh = [sem(f"s_oh{k}") for k in range(CG)]
        s_mm = sem("s_mm"); s_ev = sem("s_ev")
        s_acc = sem("s_acc"); s_h1 = sem("s_h1")
        s_m_ld = sem("s_m_ld"); s_m_tp = sem("s_m_tp"); s_m_xT = sem("s_m_xT"); s_m_mm = sem("s_m_mm")
        s_m_sq = sem("s_m_sq"); s_m_kvn = sem("s_m_kvn"); s_m_acc = sem("s_m_acc")
        s_b_out = sem("s_b_out"); s_b_st = sem("s_b_st")
        s_w = sem("s_w"); s_wc = sem("s_wc")
        s_d_o = sem("s_d_o"); s_d_tp = sem("s_d_tp"); s_d_oT = sem("s_d_oT"); s_d_mm = sem("s_d_mm")
        s_d_ld = [sem(f"s_d_ld{b}") for b in range(2)]; s_d_x1 = sem("s_d_x1"); s_d_y = sem("s_d_y")
        s_d_st = [sem(f"s_d_st{b}") for b in range(2)]
        s_d_yt = sem("s_d_yt"); s_d_yT = sem("s_d_yT"); s_d_lg = sem("s_d_lg"); s_d_lgc = sem("s_d_lgc")
        s_r_mask = sem("s_r_mask"); s_r_mm = sem("s_r_mm"); s_r_pos = sem("s_r_pos"); s_zero = sem("s_zero")
        s_zs = sem("s_zs"); s_exp = sem("s_exp"); s_x1_st = sem("s_x1_st")
        s_y_ld = [sem(f"s_y_ld{b}") for b in range(2)]; s_sc = [sem(f"s_sc{b}") for b in range(2)]; s_pi = sem("s_pi")
        s_e_w = [sem(f"s_e_w{b}") for b in range(2)]; s_e_tp = sem("s_e_tp"); s_e_yT = sem("s_e_yT")
        s_e_h = sem("s_e_h"); s_e_hT = sem("s_e_hT"); s_e_o = sem("s_e_o"); s_e_ev = sem("s_e_ev")
        s_e_st = [sem(f"s_e_st{b}") for b in range(2)]
        s_f_ld = [sem(f"s_f_ld{b}") for b in range(2)]; s_f_g = [sem(f"s_f_g{b}") for b in range(2)]
        s_f_out = sem("s_f_out"); s_f_z = sem("s_f_z"); s_f_x1 = [sem(f"s_f_x1{b}") for b in range(2)]; s_f_st = [sem(f"s_f_st{b}") for b in range(2)]

        def rows(t, i):
            return t[bass.ds(i * P, P), :]

        consts = [(srcs[:], src_t), (dsti[:], dst_t), (wts[:], wt_t),
                  (wkv[:], wkv_t.rearrange("(a p) n -> p a n", p=P)),
                  (w1t_s[:], w1t.rearrange("(a p) n -> p a n", p=P)),
                  (gw2_s[:], gw2.rearrange("(a p) n -> p a n", p=P)),
                  (wq_s[:], wq.rearrange("(a p) n -> p a n", p=P)),
                  (wo_s[:], wo_t.rearrange("(a p) n -> p a n", p=P)),
                  (kvg[:], kv_g.partition_broadcast(P)), (kvb[:], kv_b.partition_broadcast(P)),
                  (bo_s[:], bo.partition_broadcast(P)), (gam[:], gamma.partition_broadcast(P)),
                  (bet[:], beta.partition_broadcast(P)),
                  (gw[:], gate_w.rearrange("(a p) n -> p a n", p=P)),
                  (gb[:], gate_b.partition_broadcast(P))]
        CONST = 16 * len(consts)
        block = ctx.enter_context(nc.Block())

        @block.sync
        def _(sp):
            sp.dma_start(dgr[:], dst_g).then_inc(s_sch_ld, 16)

            def block_rows(t, c):
                return t[bass.ds(c * (CT * P), CT * P), :].rearrange("(q p) d -> p q d", p=P)

            def block_sb(c):
                return acc[:, bass.ds(c * (CT * D), CT * D)].rearrange("p (q d) -> p q d", d=D)

            for c in range(NC):
                sp.dma_start(block_sb(c), block_rows(x, c)).then_inc(s_x[c], 16)
            with sp.Fori(0, NC) as c:
                sp.wait_ge(s_xn, c + 1)
                sp.dma_start(block_rows(xn_d, c), block_sb(c)).then_inc(s_xst, 16)
            sp.wait_ge(s_sch, 1)
            sp.dma_start(sched_d.rearrange("(p c) m -> p c m", c=2), tiles[:]).then_inc(s_sch_st, 16)
            sp.wait_ge(s_sch_st, 16)
            sp.dma_start(trow[:], sched_d.rearrange("(o g) m -> o g m", o=1)).then_inc(s_sch_ld, 16)

            sp.wait_ge(s_xst, 16 * NC)
            sp.dma_start(xno[0][:], rows(xn_d, 0)).then_inc(s_m_ld, 16)
            with sp.Fori(1, T) as i:
                sp.wait_ge(s_m_tp, i)
                sp.dma_start(xno[0][:], rows(xn_d, i)).then_inc(s_m_ld, 16)
            sp.wait_ge(s_acc, 1)
            sp.dma_start(h1_d.rearrange("(t p) d -> p t d", p=P),
                         acc[:].rearrange("p (t d) -> p t d", d=D)).then_inc(s_h1, 16)
            sp.wait_ge(s_m_tp, T)
            sp.dma_start(xno[0][:], rows(xn_d, 0)).then_inc(s_m_ld, 16)
            sp.dma_start(xin[0][:], rows(x, 0)).then_inc(s_m_ld, 16)
            with sp.Fori(1, T) as i:
                sp.wait_ge(s_m_tp, i + T)
                sp.dma_start(xno[0][:], rows(xn_d, i)).then_inc(s_m_ld, 16)
                sp.wait_ge(s_b_out, i)
                sp.dma_start(rows(base_d, i - 1), res[0][:]).then_inc(s_b_st, 16)
                sp.dma_start(xin[0][:], rows(x, i)).then_inc(s_m_ld, 16)
            sp.wait_ge(s_b_out, T)
            sp.dma_start(base_d[(T - 1) * P:NP, :], res[0][:]).then_inc(s_b_st, 16)
            sp.wait_ge(s_b_st, 16 * T)

            def d_load(i, b):
                sp.dma_start(xin[b][:], rows(base_d, i)).then_inc(s_d_ld[b], 16)

            d_load(0, 0)
            d_load(1, 1)
            with sp.Fori(0, T // 2) as j:
                for b in range(2):
                    sp.wait_ge(s_d_x1, j * 2 + b + 1)
                    d_load(j * 2 + 2 if b == 0 else (j * 2 + 3) % T, b)
            sp.wait_ge(s_d_x1, T)
            sp.dma_start(x1_d.rearrange("(t p) d -> p t d", p=P),
                         acc[:].rearrange("p (t d) -> p t d", d=D)).then_inc(s_x1_st, 16)
            with sp.Fori(0, T // 2) as j:
                for b in range(2):
                    sp.wait_ge(s_d_y, j * 2 + b + 1)
                    sp.dma_start(rows(y_d, j * 2 + b), xno[b][:]).then_inc(s_d_st[b], 16)
            sp.wait_ge(s_d_y, T)
            sp.dma_start(rows(y_d, T - 1), xno[0][:]).then_inc(s_d_st[0], 16)
            sp.wait_ge(s_zero, 1)
            for k in range(ST // 8):
                sp.dma_start(ys_d[k * 8 * P:(k + 1) * 8 * P, :].rearrange("(p r) d -> p (r d)", p=P),
                             zero_d).then_inc(s_zs, 16)
            sp.dma_start(ys_d[(ST - ST % 8) * P:SLOTS, :], zero_d[:, 0:D]).then_inc(s_zs, 16)
            sp.wait_ge(s_d_ld[1], 16 * (T // 2 + 1))
            sp.wait_ge(s_d_st[0], 16 * (T // 2 + 1))
            sp.wait_ge(s_d_st[1], 16 * (T // 2))

            sp.wait_ge(s_r_pos, 1)
            sp.dma_start(yb[0], y_d[0:P, :]).then_inc(s_y_ld[0], 16)
            sp.dma_start(yb[1], y_d[P:2 * P, :]).then_inc(s_y_ld[1], 16)
            with sp.Fori(0, T // 2) as j:
                sp.wait_ge(s_sc[0], j * 32 + 32)
                sp.dma_start(yb[0], rows(y_d, j * 2 + 2)).then_inc(s_y_ld[0], 16)
                sp.wait_ge(s_sc[1], j * 32 + 32)
                sp.dma_start(yb[1], y_d[bass.ds((j * 2 + 3) % T * P, P), :]).then_inc(s_y_ld[1], 16)
            sp.wait_ge(s_sc[0], 32 * (T // 2 + 1))
            sp.wait_ge(s_y_ld[1], 16 * (T // 2 + 1))

            def e_load(i, b):
                e = sp.value_load(eid[0:1, bass.ds(i, 1)], min_val=0, max_val=X - 1)
                sp.dma_start(we1[b], w1[bass.ds(e, 1), :, :].rearrange("o (a p) f -> p (o a) f", p=P)
                             ).then_inc(s_e_w[b], 16)
                sp.dma_start(we2[b], w2[bass.ds(e, 1), :, :].rearrange("o (a p) f -> p (o a) f", p=P)
                             ).then_inc(s_e_w[b], 16)
                sp.dma_start(be1[b][:], b1_t[bass.ds(e, 1), :, :].rearrange("o p a -> p (o a)")
                             ).then_inc(s_e_w[b], 16)
                sp.dma_start(be2[b], b2[bass.ds(e, 1), :].rearrange("o d -> (o d)").partition_broadcast(P)
                             ).then_inc(s_e_w[b], 16)
                sp.dma_start(xno[b][:], rows(ys_d, i)).then_inc(s_e_w[b], 16)

            def e_store(i, b):
                sp.dma_start(rows(eo_d, i), eo[b]).then_inc(s_e_st[b], 16)

            e_load(0, 0)
            e_load(1, 1)
            with sp.Fori(0, ST // 2) as j:
                for b in range(2):
                    sp.wait_ge(s_e_ev, j * 2 + b + 1)
                    e_store(j * 2 + b, b)
                    e_load(j * 2 + 2 if b == 0 else (j * 2 + 3) % ST, b)
            sp.wait_ge(s_e_ev, ST)
            e_store(ST - 1, 0)
            sp.wait_ge(s_e_w[1], 80 * (ST // 2 + 1))
            sp.wait_ge(s_e_st[0], 16 * (ST // 2 + 1))
            sp.wait_ge(s_e_st[1], 16 * (ST // 2))

            sp.dma_start(xno[0][:], rows(y_d, 0)).then_inc(s_f_ld[0], 16)
            sp.dma_start(xno[1][:], rows(y_d, 1)).then_inc(s_f_ld[1], 16)
            with sp.Fori(0, T // 2) as j:
                for b in range(2):
                    sp.wait_ge(s_f_z, j * 2 + b + 1)
                    sp.dma_start(xno[b][:], rows(y_d, j * 2 + 2 if b == 0 else (j * 2 + 3) % T)
                                 ).then_inc(s_f_ld[b], 16)
            sp.dma_start(xin[0][:], rows(x1_d, 0)).then_inc(s_f_x1[0], 16)
            sp.dma_start(xin[1][:], rows(x1_d, 1)).then_inc(s_f_x1[1], 16)
            with sp.Fori(0, T // 2) as j:
                for b in range(2):
                    sp.wait_ge(s_f_out, j * 2 + b + 1)
                    sp.dma_start(rows(out, j * 2 + b), res[b][:]).then_inc(s_f_st[b], 16)
                    sp.dma_start(xin[b][:], rows(x1_d, j * 2 + 2 if b == 0 else (j * 2 + 3) % T)
                                 ).then_inc(s_f_x1[b], 16)
            sp.wait_ge(s_f_out, T)
            sp.dma_start(rows(out, T - 1), res[0][:]).then_inc(s_f_st[0], 16)
            sp.wait_ge(s_f_x1[1], 16 * (T // 2 + 1))
            sp.wait_ge(s_f_ld[1], 16 * (T // 2 + 1))
            sp.wait_ge(s_f_st[0], 16 * (T // 2 + 1))
            sp.wait_ge(s_f_st[1], 16 * (T // 2))

        @block.gpsimd
        def _(pool):
            pool.iota(iota_n[:], [[1, NP]], base=0, channel_multiplier=0,
                      allow_small_or_imprecise_dtypes=True).then_inc(s_pool, 1)
            pool.memset(ident[:], 0.0).then_inc(s_pc, 1)
            pool.memset(tri[:], 0.0).then_inc(s_pc, 1)
            pool.memset(ones[:], 1.0).then_inc(s_pool, 1)
            pool.memset(zeros[:], 0.0).then_inc(s_pool, 1)
            pool.wait_ge(s_pc, 2)
            pool.affine_select(out=ident[:], in_=ident[:], compare_op=ALU.not_equal, fill=1.0, base=0,
                               pattern=[[-1, P]], channel_multiplier=1).then_inc(s_pool, 1)
            pool.affine_select(out=tri[:], in_=tri[:], compare_op=ALU.is_ge, fill=1.0, base=0,
                               pattern=[[-1, P]], channel_multiplier=1).then_inc(s_pool, 1)
            pool.wait_ge(s_wt, CONST)
            pool.wait_ge(s_xst, 16 * NC)
            for layer in range(2):
                if layer:
                    pool.wait_ge(s_h1, 16)
                table = xn_d if layer == 0 else h1_d
                with pool.Fori(0, NI) as i:
                    for b in range(GB):
                        g = i * GB + b
                        pool.wait_ge(s_gdone, g + 1 + NG * layer)
                        pool.tensor_copy(gidx[b][:], srcs[:, bass.ds(g * CG, CG)]).then_inc(s_gx, 1)
                        pool.wait_ge(s_gx, g + 1 + NG * layer)
                        pool.nop(nofuse=True)
                        for k in range(CG):
                            pool.indirect_dma_start(gath[b][:, k, :], None, table,
                                                    bass.IndirectOffsetOnAxis(ap=gidx[b][:, k:k + 1], axis=0)
                                                    ).then_inc(s_g[b], 16)
            pool.wait_ge(s_r_pos, 1)
            pool.wait_ge(s_zs, 16 * (ST // 8 + 1))

            def scatter(i, b, n):
                pool.wait_ge(s_y_ld[b], n * 16 + 16)
                pool.tensor_copy(pidx[b][:], pos[:, bass.ds(i, 1), :].rearrange("p o k -> p (o k)")
                                 ).then_inc(s_pi, 1)
                pool.wait_ge(s_pi, i + 1)
                pool.nop(nofuse=True)
                for k in range(2):
                    pool.indirect_dma_start(ys_d, bass.IndirectOffsetOnAxis(ap=pidx[b][:, k:k + 1], axis=0),
                                            yb[b], None).then_inc(s_sc[b], 16)

            with pool.Fori(0, T // 2) as j:
                for b in range(2):
                    scatter(j * 2 + b, b, j)
            scatter(T - 1, 0, T // 2)
            pool.wait_ge(s_e_st[0], 16 * (ST // 2 + 1))
            pool.wait_ge(s_e_st[1], 16 * (ST // 2))
            pool.wait_ge(s_sc[0], 32 * (T // 2 + 1))

            def collect(i, b):
                pool.wait_ge(s_f_z, i - 1)
                pool.tensor_copy(pidx[b][:], pos[:, bass.ds(i, 1), :].rearrange("p o k -> p (o k)")
                                 ).then_inc(s_pi, 1)
                pool.wait_ge(s_pi, i + 1 + T)
                pool.nop(nofuse=True)
                for k in range(2):
                    pool.indirect_dma_start(yb[2 * b + k], None, eo_d,
                                            bass.IndirectOffsetOnAxis(ap=pidx[b][:, k:k + 1], axis=0)
                                            ).then_inc(s_f_g[b], 16)
            for i in range(2):
                if i == 0:
                    pool.wait_ge(s_e_w[1], 80 * (ST // 2 + 1))
                pool.tensor_copy(pidx[i][:], pos[:, i, :]).then_inc(s_pi, 1)
                pool.wait_ge(s_pi, i + 1 + T)
                for k in range(2):
                    pool.indirect_dma_start(yb[2 * i + k], None, eo_d,
                                            bass.IndirectOffsetOnAxis(ap=pidx[i][:, k:k + 1], axis=0)
                                            ).then_inc(s_f_g[i], 16)
            with pool.Fori(1, T // 2) as j:
                for b in range(2):
                    collect(j * 2 + b, b)
            collect(T - 1, 0)

        @block.scalar
        def _(act):
            for dst, s in consts:
                act.dma_start(dst, s).then_inc(s_wt, 16)
            for c in range(NC):
                act.wait_ge(s_xv, c + 1)
                a = sda[:, c * CT:(c + 1) * CT]
                act.activation(a, a, ACT.Sqrt).then_inc(s_xs, 1)
            with act.Fori(0, T) as i:
                act.wait_ge(s_m_tp, i + 1)
                act.activation(xT[0][:], bank[1][:, 0:D].rearrange("p (a q) -> p a q", a=2), ACT.Copy
                               ).then_inc(s_m_xT, 1)
                act.wait_ge(s_m_mm, i + 1)
                act.activation(sq[:], bank[2][:], ACT.Square).then_inc(s_m_sq, 1)
                act.wait_ge(s_m_var, i + 1)
                act.activation(r8[:, 1, :], r8[:, 0, :], ACT.Sqrt).then_inc(s_m_sd, 1)
            with act.Fori(0, T) as i:
                act.wait_ge(s_m_tp, i + 1 + T)
                act.wait_ge(s_m_mm, i + T)
                act.activation(xT[0][:], bank[1][:, 0:D].rearrange("p (a q) -> p a q", a=2), ACT.Copy
                               ).then_inc(s_m_xT, 1)

            def sums_tile(i, b, n):
                act.activation(hot2[b], acc[:, bass.ds(i * D, D)], ACT.Copy).then_inc(s_d_o, 1)
                act.wait_ge(s_d_tp, i + 1)
                wait_from(act, s_d_mm, i - 1)
                act.activation(xT[b][:], bank[b][:, 0:D].rearrange("p (a q) -> p a q", a=2), ACT.Copy
                               ).then_inc(s_d_oT, 1)

            def y_tile(i, b, n):
                act.wait_ge(s_d_yt, i + 1)
                wait_from(act, s_d_lg, i - 1)
                act.activation(yT[b][:], bank[4 + b][:, 0:D].rearrange("p (a q) -> p a q", a=2), ACT.Copy
                               ).then_inc(s_d_yT, 1)

            act.wait_ge(s_acc, 2)
            in_pairs(act, T, sums_tile)
            act.wait_ge(s_xv, NC + 1)
            act.activation(sda[:], sda[:], ACT.Sqrt).then_inc(s_xs, 1)
            in_pairs(act, T, y_tile)
            act.wait_ge(s_r_pos, 1)
            act.activation(pw[1][:], pw[1][:], ACT.Exp).then_inc(s_exp, 1)

            def e_tile(i, b, n):
                act.wait_ge(s_e_tp, i + 1)
                act.activation(yT[b][:], bank[b][:, 0:D].rearrange("p (a q) -> p a q", a=2), ACT.Copy
                               ).then_inc(s_e_yT, 1)
                act.wait_ge(s_e_h, i + 1)
                wait_from(act, s_e_o, i - 1)
                for f in range(4):
                    ins = act.activation(hT[b][:, f, :], bank[2 + b][:, f * P:(f + 1) * P], ACT.Relu,
                                         bias=be1[b][:, f:f + 1])
                ins.then_inc(s_e_hT, 1)

            in_pairs(act, ST, e_tile)
            act.wait_ge(s_xv, NC + 2)
            act.activation(sda[:], sda[:], ACT.Sqrt).then_inc(s_xs, 1)

        @block.tensor
        def _(pe):
            def transpose(ps, row_tile, signal):
                for a in range(2):
                    ins = pe.transpose(ps[:, a * P:(a + 1) * P], row_tile[:, a * P:(a + 1) * P], ident[:])
                ins.then_inc(signal, 1)

            pe.wait_ge(s_wt, CONST)
            pe.wait_ge(s_pool, 5)
            for i in range(2):
                for a in range(2):
                    ins = pe.matmul(bank[4 + i][:, 0:D], w1t_s[:, a, i * P:(i + 1) * P], gw2_s[:, a, :],
                                    start=a == 0, stop=a == 1)
            ins.then_inc(s_w, 1)
            for p in range(2):
                pe.matmul(bank[3][:, p * P:(p + 1) * P], zeros[:], zeros[:], start=p == 0, stop=False,
                          skip_group_check=True)
            pe.wait_ge(s_tab, 1)
            pe.wait_ge(s_wc, 1)

            def kv_proj(i):
                pe.wait_ge(s_m_ld, i * 16 + 16)
                transpose(bank[1], xno[0], s_m_tp)
                pe.wait_ge(s_m_xT, i + 1)
                for a in range(2):
                    ins = pe.matmul(bank[2][:], xT[0][:, a, :], wkv[:, a, :], start=a == 0, stop=a == 1)
                ins.then_inc(s_m_mm, 1)

            def kv_sum(i, m):
                pe.wait_ge(s_m_kvn, i + 1)
                for p in range(2):
                    ins = pe.matmul(bank[3][:, p * P:(p + 1) * P], kvn[0:m, D + p * P:D + (p + 1) * P],
                                    kvn[0:m, p * P:(p + 1) * P], start=False, stop=False, skip_group_check=True)
                ins.then_inc(s_m_acc, 1)

            def base_rows(i):
                pe.wait_ge(s_m_ld, i * 32 + (16 * T + 32))
                transpose(bank[1], xno[0], s_m_tp)
                pe.wait_ge(s_m_xT, i + 1 + T)
                wait_from(pe, s_b_out, i)
                for a in range(2):
                    ins = pe.matmul(bank[2][:, 0:D], xT[0][:, a, :], mixm[:, a, :], start=a == 0, stop=a == 1)
                ins.then_inc(s_m_mm, 1)

            def sum_group(i, b, layer):
                row = bass.ds(i * GB + b + NG * layer, 1)
                before = pe.value_load(tab[0:1, row, 0], min_val=0, max_val=STEPS)
                after = pe.value_load(tab[0:1, row, 1], min_val=1, max_val=STEPS)
                with pe.Fori(before, after) as step:
                    pe.wait_ge(s_g[b], i * (16 * CG) + 16 * CG * (1 + NI * layer))
                    pe.wait_ge(s_ev, step + 1)
                    for k in range(CG):
                        pe.wait_ge(s_oh[k], step + 1)
                        ins = pe.matmul(bank[0][:, 0:D], hot[k][:], gath[b][:, k, :], start=k == 0,
                                        stop=k == CG - 1)
                    ins.then_inc(s_mm, 1)

            def edge_turn(i, layer, last):
                for b in range(GB):
                    sum_group(i, b, layer)
                    if b == 0:
                        if layer == 0:
                            kv_proj(i)
                        else:
                            base_rows(i)
                    if b == 2 and layer == 0:
                        kv_sum(i, N - (T - 1) * P if last else P)

            with pe.Fori(0, NI - 1) as i:
                edge_turn(i, 0, False)
            edge_turn(NI - 1, 0, True)
            pe.wait_ge(s_wc, 2)
            for p in range(2):
                ins = pe.matmul(bank[4 + p][:, 0:D], kvT[:, p, :], wo_s[:, p, :], start=True, stop=True)
            ins.then_inc(s_w, 1)
            pe.wait_ge(s_wc, 3)
            for i in range(2):
                for p in range(2):
                    ins = pe.matmul(bank[6 + i][:, 0:D], wq_s[:, p, i * P:(i + 1) * P], t1[:, p, :],
                                    start=p == 0, stop=p == 1)
            ins.then_inc(s_w, 1)
            pe.wait_ge(s_wc, 4)
            edge_turn(0, 1, False)
            with pe.Fori(1, NI) as i:
                edge_turn(i, 1, False)

            def sums_tile(i, b, n):
                pe.wait_ge(s_d_o, i + 1)
                transpose(bank[b], hot2[b], s_d_tp)
                pe.wait_ge(s_d_oT, i + 1)
                wait_from(pe, s_d_x1, i - 1)
                for a in range(2):
                    ins = pe.matmul(bank[2 + b][:, 0:D], xT[b][:, a, :], w12[:, a, :], start=a == 0, stop=a == 1)
                ins.then_inc(s_d_mm, 1)

            def y_tile(i, b, n):
                pe.wait_ge(s_d_y, i + 1)
                transpose(bank[4 + b], xno[b], s_d_yt)
                pe.wait_ge(s_d_yT, i + 1)
                wait_from(pe, s_d_lgc, i - 1)
                for a in range(2):
                    ins = pe.matmul(bank[6 + b][:, 0:X], yT[b][:, a, :], gw[:, a, :], start=a == 0, stop=a == 1)
                ins.then_inc(s_d_lg, 1)

            in_pairs(pe, T, sums_tile)
            in_pairs(pe, T, y_tile)
            pe.wait_ge(s_r_mask, 1)
            half = n_r // 2
            for h in range(2):
                pe.matmul(bank[h][:, 0:half], tri[:], rt(0)[:, h * half:(h + 1) * half], start=True, stop=True)
                ins = pe.matmul(bank[2 + h][:, 0:half], ones[:], rt(0)[:, h * half:(h + 1) * half],
                                start=True, stop=True)
            ins.then_inc(s_r_mm, 1)

            def e_tile(i, b, n):
                pe.wait_ge(s_e_w[b], n * 80 + 80)
                transpose(bank[b], xno[b], s_e_tp)
                pe.wait_ge(s_e_yT, i + 1)
                for f in range(4):
                    for a in range(2):
                        ins = pe.matmul(bank[2 + b][:, f * P:(f + 1) * P], we1[b][:, a, f * P:(f + 1) * P],
                                        yT[b][:, a, :], start=a == 0, stop=a == 1)
                ins.then_inc(s_e_h, 1)
                pe.wait_ge(s_e_hT, i + 1)
                wait_from(pe, s_e_ev, i - 1)
                for f in range(4):
                    ins = pe.matmul(bank[4 + b][:, 0:D], hT[b][:, f, :], we2[b][:, f, :], start=f == 0,
                                    stop=f == 3)
                ins.then_inc(s_e_o, 1)

            pe.wait_ge(s_r_pos, 1)
            in_pairs(pe, ST, e_tile)

        @block.vector
        def _(dve):
            own = Links(dve, s_dve)
            link = own.link

            def stats(t, src):
                link(dve.bn_stats(st6[:], src))
                dve.nop(nofuse=True)
                link(dve.bn_aggr(mv[:], st6[:]))
                link(dve.tensor_copy(mva[:, t, :] if isinstance(t, int) else
                                     mva[:, bass.ds(t, 1), :].rearrange("p o m -> p (o m)"), mv[:]))

            def col(a, t):
                return a[:, t:t + 1] if isinstance(t, int) else a[:, bass.ds(t, 1)]

            def mean(t):
                return mva[:, t, 0:1] if isinstance(t, int) else mva[:, bass.ds(t, 1), 0]

            def normed(dst, src, t):
                return dve.tensor_scalar(dst, src, mean(t), col(rsa, t), ALU.subtract, ALU.mult)

            def deviations(t0, n, ready, rooted, at):
                dve.tensor_scalar(sda[:, t0:t0 + n], mva[:, t0:t0 + n, 1], EPS, None, ALU.add).then_inc(ready, 1)
                dve.wait_ge(rooted, at)
                link(dve.reciprocal(rsa[:, t0:t0 + n], sda[:, t0:t0 + n]))

            dve.wait_ge(s_sch_ld, 16)
            link(dve.tensor_reduce(mnmx[:, :, 0], dgr[:], AX.X, ALU.min))
            link(dve.tensor_reduce(mnmx[:, :, 1], dgr[:], AX.X, ALU.max))
            dve.tensor_scalar(tiles[:], mnmx[:], 7, None, ALU.arith_shift_right).then_inc(s_sch, 1)

            for c in range(NC):
                dve.wait_ge(s_x[c], 16)
                for q in range(CT):
                    t = c * CT + q
                    stats(t, acc[:, t * D:(t + 1) * D])
                deviations(c * CT, CT, s_xv, s_xs, c + 1)
                for q in range(CT):
                    t = c * CT + q
                    a = acc[:, t * D:(t + 1) * D]
                    link(normed(a, a, t))
                dve.memset(scr[:, 0:1], 0.0).then_inc(s_xn, 1)

            dve.wait_ge(s_wt, CONST)
            link(dve.tensor_copy(dstf[:], dsti[:]))
            wv = wkv[:].rearrange("p a (h c) -> p (a h) c", c=HD)
            link(dve.tensor_reduce(hsum[:], wv, AX.X, ALU.add))
            link(dve.tensor_scalar(hsum[:], hsum[:], 1.0 / HD, None, ALU.mult))
            link(dve.tensor_tensor(wv, wv, hsum[:].unsqueeze(2).broadcast_to([P, 2 * H2, HD]), ALU.subtract))
            dve.wait_ge(s_w, 1)
            for i in range(2):
                link(dve.tensor_copy(w12[:, i, :], bank[4 + i][:, 0:D]))
            link(dve.memset(one_row[:], 1.0))
            dve.wait_ge(s_sch_ld, 32)
            tb = tab[:].rearrange("o (l g) m -> o l g m", l=2)
            link(dve.tensor_tensor(cnt[:], trow[:, :, 1], trow[:, :, 0], ALU.subtract))
            link(dve.tensor_scalar(cnt[:], cnt[:], 1.0, None, ALU.add))
            link(dve.tensor_tensor_scan(cum[:], one_row[:], cnt[:], 0.0, ALU.mult, ALU.add))
            link(dve.tensor_copy(tb[:, 0, :, 1], cum[:]))
            link(dve.tensor_tensor(tb[:, 0, :, 0], cum[:], cnt[:], ALU.subtract))
            for c in range(2):
                link(dve.tensor_scalar(tb[:, 1, :, c], tb[:, 0, :, c], cum[:, NG - 1:NG], None, ALU.add))
            for l in range(2):
                link(dve.tensor_tensor(tb[:, l, :, 2], trow[:, :, 0], tb[:, l, :, 0], ALU.subtract))
            for l in range(2):
                link(dve.tensor_scalar(tb[:, l, :, 2], tb[:, l, :, 2], float(STEPS), None, ALU.add))
            dve.memset(scr[:, 5:6], 0.0).then_inc(s_tab, 1)
            dve.wait_ge(s_tab, 1)
            link(dve.memset(kvT[:], 0.0))
            for k in range(GB):
                link(dve.memset(scr[:, 0:1], 0.0))
                dve.memset(scr[:, 1:2], 0.0).then_inc(s_gdone, 1)
                dve.wait_ge(s_gdone, k + 1)
            dve.wait_ge(s_xst, 16 * NC)
            link(dve.memset(acc[:], 0.0))
            dve.memset(scr[:, 2:3], 0.0).then_inc(s_ev, 1)
            dve.memset(scr[:, 3:4], 0.0).then_inc(s_wc, 1)
            dve.wait_ge(s_pool, 5)
            dve.wait_ge(s_wc, 1)

            def sum_group(i, b, layer):
                g = i * GB + b
                row = bass.ds(g + NG * layer, 1)
                before = dve.value_load(tab[0:1, row, 0], min_val=0, max_val=STEPS)
                after = dve.value_load(tab[0:1, row, 1], min_val=1, max_val=STEPS)
                shift = dve.value_load(tab[0:1, row, 2], min_val=0, max_val=STEPS + T)
                with dve.Fori(before, after) as step:
                    t_in = nc.s_assert_within(step + shift - STEPS, 0, T - 1,
                                              skip_runtime_bounds_check_because="it is a tile number")
                    for k in range(CG):
                        c = g * CG + k
                        dve.tensor_scalar(hot[k][:], iota_n[:, bass.ds(t_in * P, P)], dstf[:, bass.ds(c, 1)],
                                          wts[:, bass.ds(c, 1)], ALU.is_equal, ALU.mult).then_inc(s_oh[k], 1)
                    dve.wait_ge(s_ev, step + 1)
                    dve.wait_ge(s_mm, step + 1)
                    a = acc[:, bass.ds(t_in * D, D)]
                    dve.tensor_tensor(a, bank[0][:, 0:D], a, ALU.add).then_inc(s_ev, 1)
                    dve.wait_ge(s_ev, step + 2)
                dve.memset(scr[:, 4:5], 0.0).then_inc(s_gdone, 1)
                dve.wait_ge(s_gdone, g + (1 + GB) + NG * layer)

            def kv_norm(i):
                dve.wait_ge(s_m_sq, i + 1)
                link(dve.tensor_reduce(r8[:, 0, :], sq[:].rearrange("p (h c) -> p h c", c=HD), AX.X, ALU.add))
                dve.tensor_scalar(r8[:, 0, :], r8[:, 0, :], 1.0 / HD, EPS, ALU.mult, ALU.add).then_inc(s_m_var, 1)
                dve.wait_ge(s_m_sd, i + 1)
                link(dve.reciprocal(r8[:, 1, :], r8[:, 1, :]))
                if not isinstance(i, int):
                    dve.wait_ge(s_m_acc, i)
                link(dve.tensor_tensor(kvn[:].rearrange("p (h c) -> p h c", c=HD),
                                       bank[2][:].rearrange("p (h c) -> p h c", c=HD),
                                       r8[:, 1, :].unsqueeze(2).broadcast_to([P, H2, HD]), ALU.mult))
                link(dve.tensor_tensor(kvn[:], kvn[:], kvg[:], ALU.mult))
                dve.tensor_tensor(kvn[:], kvn[:], kvb[:], ALU.add).then_inc(s_m_kvn, 1)

            def base_add(i):
                dve.wait_ge(s_m_mm, i + (1 + T))
                dve.wait_ge(s_m_ld, i * 32 + (16 * T + 32))
                if not isinstance(i, int):
                    dve.wait_ge(s_b_st, i * 16)
                link(dve.tensor_tensor(res[0][:], bank[2][:, 0:D], xin[0][:], ALU.add))
                dve.tensor_tensor(res[0][:], res[0][:], bo_s[:], ALU.add).then_inc(s_b_out, 1)

            def edge_turn(i, layer):
                for b in range(GB):
                    sum_group(i, b, layer)
                    if b == 1:
                        if layer == 0:
                            kv_norm(i)
                        else:
                            base_add(i)

            for b in range(GB):
                sum_group(0, b, 0)
                if b == 1:
                    kv_norm(0)
            own.enter()
            with dve.Fori(1, NI) as i:
                own.turn(i - 1, 4)
                edge_turn(i, 0)
            own.leave(NI - 1, 4)
            dve.memset(scr[:, 5:6], 0.0).then_inc(s_acc, 1)
            dve.wait_ge(s_m_acc, T)
            for h in range(4):
                p, o = h // 2, (h % 2) * HD
                link(dve.tensor_scalar(kvT[o:o + HD, p, o:o + HD], bank[3][o:o + HD, p * P + o:p * P + o + HD],
                                       1.0 / N, None, ALU.mult))
            dve.memset(scr[:, 6:7], 0.0).then_inc(s_wc, 1)
            dve.wait_ge(s_w, 2)
            for p in range(2):
                link(dve.tensor_copy(t1[:, p, :], bank[4 + p][:, 0:D]))
            dve.memset(scr[:, 7:8], 0.0).then_inc(s_wc, 1)
            dve.wait_ge(s_w, 3)
            for p in range(2):
                link(dve.tensor_copy(mixm[:, p, :], bank[6 + p][:, 0:D]))
            dve.wait_ge(s_h1, 16)
            link(dve.memset(acc[:], 0.0))
            dve.memset(scr[:, 6:7], 0.0).then_inc(s_wc, 1)
            for b in range(GB):
                sum_group(0, b, 1)
                if b == 1:
                    base_add(0)
            own.enter()
            with dve.Fori(1, NI) as i:
                own.turn(i - 1, 1)
                edge_turn(i, 1)
            own.leave(NI - 1, 1)
            dve.memset(scr[:, 5:6], 0.0).then_inc(s_acc, 1)
            link(dve.memset(zero_d, 0.0))
            dve.memset(scr[:, 4:5], 0.0).then_inc(s_zero, 1)

            dve.wait_ge(s_b_st, 16 * T)

            def x1_tile(i, b, n):
                dve.wait_ge(s_d_mm, i + 1)
                dve.wait_ge(s_d_ld[b], n * 16 + 16)
                link(dve.tensor_tensor(res[b][:], bank[2 + b][:, 0:D], xin[b][:], ALU.add))
                dve.tensor_copy(acc[:, bass.ds(i * D, D)], res[b][:]).then_inc(s_d_x1, 1)
                stats(i, res[b][:])

            own.enter()
            with dve.Fori(0, T // 2) as j:
                own.turn(j, 8)
                for b in range(2):
                    x1_tile(j * 2 + b, b, j)
            own.leave(T // 2, 8)
            x1_tile(T - 1, 0, T // 2)
            deviations(0, T, s_xv, s_xs, NC + 1)

            def y_tile(i, b):
                normed(xno[b][:], acc[:, bass.ds(i * D, D)], i).then_inc(s_d_y, 1)

            def logits(i, b):
                dve.wait_ge(s_d_lg, i + 1)
                dve.tensor_tensor(lg[:, bass.ds(i * X, X)], bank[6 + b][:, 0:X], gb[:], ALU.add
                                  ).then_inc(s_d_lgc, 1)

            for b in range(2):
                y_tile(b, b)
            with dve.Fori(1, T // 2) as j:
                for b in range(2):
                    logits(j * 2 + b - 2, b)
                    dve.wait_ge(s_d_st[b], j * 16)
                    y_tile(j * 2 + b, b)
            logits(T - 3, 0)
            dve.wait_ge(s_d_st[0], 16 * (T // 2))
            y_tile(T - 1, 0)
            logits(T - 2, 1)
            logits(T - 1, 0)
            dve.wait_ge(s_x1_st, 16)
            dve.wait_ge(s_d_lgc, T)

            def v3(ap):
                return ap.rearrange("p (t e) -> p t e", e=X)

            def per_t(ap):
                return ap.unsqueeze(2).broadcast_to([P, T, X])

            def per_e(ap):
                return ap.unsqueeze(1).broadcast_to([P, T, X])

            link(dve.tensor_copy(iota_x[:], iota_n[:, 0:X]))
            cur = lg[:]
            for k in range(2):
                link(dve.tensor_reduce(mx[k][:], v3(cur), AX.X, ALU.max))
                link(dve.tensor_tensor(v3(rt(1)), v3(cur), per_t(mx[k][:]), ALU.not_equal))
                link(dve.tensor_scalar(rt(1), rt(1), float(X), None, ALU.mult))
                link(dve.tensor_tensor(v3(rt(1)), v3(rt(1)), per_e(iota_x[:]), ALU.add))
                link(dve.tensor_reduce(ix[k][:], v3(rt(1)), AX.X, ALU.min))
                link(dve.tensor_tensor(v3(rt(2 + k)), per_e(iota_x[:]), per_t(ix[k][:]), ALU.is_equal))
                if k == 0:
                    link(dve.tensor_scalar(rt(4), rt(2), -3.0e38, None, ALU.mult))
                    link(dve.tensor_scalar(rt(5), rt(2), -1.0, 1.0, ALU.mult, ALU.add))
                    link(dve.tensor_tensor(rt(5), rt(5), lg[:], ALU.mult))
                    link(dve.tensor_tensor(rt(6), rt(4), rt(5), ALU.add))
                    cur = rt(6)
            dve.tensor_tensor(rt(0), rt(2), rt(3), ALU.add).then_inc(s_r_mask, 1)
            dve.wait_ge(s_r_mm, 1)
            half = n_r // 2
            for h in range(2):
                link(dve.tensor_copy(rt(7)[:, h * half:(h + 1) * half], bank[2 + h][:, 0:half]))
                link(dve.tensor_copy(rt(8)[:, h * half:(h + 1) * half], bank[h][:, 0:half]))
            tot_e = rt(9).rearrange("p (e t) -> p e t", t=T)
            link(dve.tensor_copy(tot_e, rt(7).rearrange("p (t e) -> p e t", e=X)))
            link(dve.memset(rt(10), 1.0))
            link(dve.memset(rt(10).rearrange("p (e t) -> p e t", t=T)[:, :, 0], 0.0))
            link(dve.tensor_tensor_scan(rt(11), rt(10), rt(9), 0.0, ALU.mult, ALU.add))
            run_e = rt(11).rearrange("p (e t) -> p e t", t=T)
            link(dve.tensor_scalar(nt_i[:], run_e[:, :, T - 1], float(P - 1), None, ALU.add))
            link(dve.tensor_scalar(nt_i[:], nt_i[:], 7, None, ALU.arith_shift_right))
            link(dve.tensor_copy(nt_f[:, 0, :], nt_i[:]))
            link(dve.tensor_tensor_scan(nt_f[:, 1, :], ones[:, 0:X], nt_f[:, 0, :], 0.0, ALU.mult, ALU.add))
            link(dve.tensor_tensor(nt_f[:, 2, :], nt_f[:, 1, :], nt_f[:, 0, :], ALU.subtract))
            link(dve.tensor_tensor(rt(11), rt(11), rt(9), ALU.subtract))
            link(dve.tensor_tensor(v3(rt(8)), v3(rt(8)), rt(11).rearrange("p (e t) -> p t e", t=T), ALU.add))
            link(dve.tensor_scalar(nt_f[:, 2, :], nt_f[:, 2, :], float(P), None, ALU.mult))
            link(dve.tensor_tensor(v3(rt(8)), v3(rt(8)), per_e(nt_f[:, 2, :]), ALU.add))
            for k in range(2):
                link(dve.tensor_tensor(rt(1), rt(8), rt(2 + k), ALU.mult))
                link(dve.tensor_reduce(posf[:, :, k], v3(rt(1)), AX.X, ALU.add))
            link(dve.tensor_copy(pos[:], posf[:]))
            sel = acc[0:1, 0:ST * X].rearrange("o (i e) -> o i e", e=X)
            link(dve.tensor_tensor(sel, iota_n[0:1, 0:ST].unsqueeze(2).broadcast_to([1, ST, X]),
                                   nt_f[0:1, 1, :].unsqueeze(1).broadcast_to([1, ST, X]), ALU.is_ge))
            link(dve.tensor_reduce(cnt[:, 0:ST], sel, AX.X, ALU.add))
            link(dve.tensor_scalar(eid[:], cnt[:, 0:ST], float(X - 1), None, ALU.min))
            link(dve.tensor_tensor(pw[1][:], mx[1][:], mx[0][:], ALU.subtract))
            dve.memset(scr[:, 3:4], 0.0).then_inc(s_r_pos, 1)
            dve.wait_ge(s_exp, 1)
            link(dve.tensor_scalar(pw[0][:], pw[1][:], 1.0, None, ALU.add))
            link(dve.reciprocal(pw[0][:], pw[0][:]))
            link(dve.tensor_tensor(pw[1][:], pw[1][:], pw[0][:], ALU.mult))

            def e_tile(i, b, n):
                dve.wait_ge(s_e_o, i + 1)
                dve.tensor_tensor(eo[b], bank[4 + b][:, 0:D], be2[b], ALU.add).then_inc(s_e_ev, 1)

            for b in range(2):
                e_tile(b, b, 0)
            with dve.Fori(1, ST // 2) as j:
                for b in range(2):
                    dve.wait_ge(s_e_st[b], j * 16)
                    e_tile(j * 2 + b, b, j)
            dve.wait_ge(s_e_st[0], 16 * (ST // 2))
            e_tile(ST - 1, 0, ST // 2)

            def z_tile(i, b, n):
                dve.wait_ge(s_f_ld[b], n * 16 + 16)
                dve.wait_ge(s_f_g[b], n * 32 + 32)
                link(dve.scalar_tensor_tensor(out=xno[b][:], in0=yb[2 * b], scalar=col(pw[0], i),
                                              in1=xno[b][:], op0=ALU.mult, op1=ALU.add))
                link(dve.scalar_tensor_tensor(out=res[b][:], in0=yb[2 * b + 1], scalar=col(pw[1], i),
                                              in1=xno[b][:], op0=ALU.mult, op1=ALU.add))
                dve.tensor_copy(acc[:, bass.ds(i * D, D)], res[b][:]).then_inc(s_f_z, 1)
                stats(i, res[b][:])

            own.enter()
            with dve.Fori(0, T // 2) as j:
                own.turn(j, 10)
                for b in range(2):
                    z_tile(j * 2 + b, b, j)
            own.leave(T // 2, 10)
            z_tile(T - 1, 0, T // 2)
            deviations(0, T, s_xv, s_xs, NC + 2)

            def out_tile(i, b, n):
                dve.wait_ge(s_f_x1[b], n * 16 + 16)
                a = acc[:, bass.ds(i * D, D)]
                link(normed(res[b][:], a, i))
                link(dve.tensor_tensor(res[b][:], res[b][:], gam[:], ALU.mult))
                link(dve.tensor_tensor(xin[b][:], xin[b][:], bet[:], ALU.add))
                dve.tensor_tensor(res[b][:], res[b][:], xin[b][:], ALU.add).then_inc(s_f_out, 1)

            for b in range(2):
                out_tile(b, b, 0)
            own.enter()
            with dve.Fori(1, T // 2) as j:
                own.turn(j - 1, 6)
                for b in range(2):
                    dve.wait_ge(s_f_st[b], j * 16)
                    out_tile(j * 2 + b, b, j)
            own.leave(T // 2 - 1, 6)
            dve.wait_ge(s_f_st[0], 16 * (T // 2))
            out_tile(T - 1, 0, T // 2)


def kernel(**inputs):
    import numpy as np
    import concourse.bacc as bacc
    from concourse.bass_utils import run_bass_kernel_spmd as run

    def pad(a, value):
        return np.concatenate([np.asarray(a), np.full((EP - E,), value, np.asarray(a).dtype)])

    def columns(a):
        return np.ascontiguousarray(a.reshape(NCH, P).T)

    f = {k: np.asarray(v) for k, v in inputs.items()}
    dst = pad(f["dst"], N - 1)
    arrays = {
        "x": np.concatenate([f["x"], np.zeros((NP - N, D), np.float32)]),
        "src_t": columns(pad(f["src"], 0)),
        "dst_t": columns(dst),
        "dst_g": dst.reshape(DG, 2, P * CG),
        "wt_t": columns(pad(f["edge_weight"], 0)),
        "w1t": f["L0_gnn_W1"].T,
        "gw2": f["L0_gnn_W2"],
        "wq": f["L0_mix_wq"],
        "wkv_t": np.concatenate([f["L0_mix_wk"], f["L0_mix_wv"]]).T,
        "wo_t": f["L0_mix_wo"].T,
        "bo": f["L0_mix_bo"],
        "kv_g": np.concatenate([f["L0_mix_ln_k_g"]] * 4 + [f["L0_mix_ln_v_g"]] * 4),
        "kv_b": np.concatenate([f["L0_mix_ln_k_b"]] * 4 + [f["L0_mix_ln_v_b"]] * 4),
        "gate_w": f["L0_ffn_gate_w"],
        "gate_b": f["L0_ffn_gate_b"],
        "w1": f["L0_ffn_w1"],
        "b1_t": f["L0_ffn_b1"].reshape(X, FF // P, P).transpose(0, 2, 1),
        "w2": f["L0_ffn_w2"],
        "b2": f["L0_ffn_b2"],
        "gamma": f["L0_ffn_gamma"],
        "beta": f["L0_ffn_beta"],
    }
    nc = bacc.Bacc("TRN2", target_bir_lowering=False, num_devices=1)
    given, args = {}, []
    for name, a in arrays.items():
        a = np.ascontiguousarray(a)
        given[f"in_{name}"] = a
        args.append(nc.dram_tensor(f"in_{name}", a.shape, mybir.dt.from_np(a.dtype), kind="ExternalInput").ap())
    args.append(nc.dram_tensor("out_rows", (NP, D), F32, kind="ExternalOutput").ap())
    gps_layer(nc, *args)
    r = run(nc, [given], core_ids=[0])
    return r.results[0]["out_rows"][:N]
```

```python
from contextlib import ExitStack

import concourse.bass as bass
from concourse import mybir

F32 = mybir.dt.float32
I32 = mybir.dt.int32
U32 = mybir.dt.uint32
ALU = mybir.AluOpType
ACT = mybir.ActivationFunctionType
AX = mybir.AxisListType

P = 128
N = 6250
D = 256
E = 200000
T = -(-N // P)
NP = T * P
HD = 64
H2 = 2 * D // HD
CG = 8
GB = 4
NG = -(-E // (P * CG * GB)) * GB
NCH = NG * CG
EP = NCH * P
NI = NG // GB
X = 16
FF = 512
ST = (2 * NP) // P + X - 1
SLOTS = ST * P
RW = D + 4
NONE = 2 * NP
EPS = 1e-5
STEPS = 2 * NG * T
CT = 7
NC = T // CT
assert NC * CT == T
assert NI == T and T % 2 == 1 and ST % 2 == 1
DG = NG // 2


class Links:

    def __init__(self, eng, sem):
        self.eng, self.sem, self.at, self.n = eng, sem, 0, 0

    def link(self, ins):
        ins.then_inc(self.sem, 1)
        self.n += 1
        self.eng.wait_ge(self.sem, self.at + self.n)

    def post(self, ins):
        ins.then_inc(self.sem, 1)
        self.n += 1

    def until(self, back):
        self.eng.wait_ge(self.sem, self.at + (self.n - back))

    def turn(self, i, per):
        self.at = self.base + i * per
        self.n = 0

    def enter(self):
        self.base = self.at + self.n

    def leave(self, turns, per):
        assert self.n == per, self.n
        self.at, self.n = self.base + turns * per, 0


def in_pairs(eng, n, tile):
    for b in range(2):
        tile(b, b, 0)
    with eng.Fori(1, n // 2) as j:
        for b in range(2):
            tile(j * 2 + b, b, j)
    tile(n - 1, 0, n // 2)


def in_turns(eng, n, slots, tile):
    for b in range(slots):
        tile(b, b, 0)
    with eng.Fori(1, n // slots) as j:
        for b in range(slots):
            tile(j * slots + b, b, j)
    for i in range(n // slots * slots, n):
        tile(i, i % slots, i // slots)


def wait_from(eng, sem, value):
    if not isinstance(value, int) or value > 0:
        eng.wait_ge(sem, value)


def gps_layer(nc, x, src_t, dst_t, dst_g, wt_t, w1t, gw2, wq, wkv_t, wo_t, bo, kv_g, kv_b,
              gate_w, gate_b, w1, b1_t, w2, b2, gamma, beta, out):
    with ExitStack() as ctx:
        def sb(name, shape, dt=F32):
            return ctx.enter_context(nc.sbuf_tensor(name, shape, dt))

        def sem(name):
            return ctx.enter_context(nc.semaphore(name))

        def dram(name, shape, dt=F32):
            return nc.dram_tensor(name, shape, dt, kind="Internal").ap()

        sums = ctx.enter_context(nc.psum_tensor("sums", [P, 1024], F32))
        bank = [ctx.enter_context(nc.psum_tensor(f"bank{n}", [P, 512], F32)) for n in range(1, 7)]
        bank = [sums[:, 0:512]] + [t[:] for t in bank] + [sums[:, 512:1024]]

        xn_d = dram("xn_d", [NP, D])
        h1_d = dram("h1_d", [NP, D])
        base_d = dram("base_d", [NP, D])
        x1_d = dram("x1_d", [NP, D])
        y_d = dram("y_d", [NP, D])
        sched_d = dram("sched_d", [NG, 2], I32)
        ys_d = dram("ys_d", [SLOTS, RW])
        eo_d = dram("eo_d", [2 * NP, D])

        srcs = sb("srcs", [P, NCH + GB * CG], I32)
        dsti = sb("dsti", [P, NCH], I32)
        dstf = sb("dstf", [P, NCH])
        wts = sb("wts", [P, NCH])
        dgr = sb("dgr", [DG, 2, P * CG], I32)
        mnmx = sb("mnmx", [DG, 2, 2], I32)
        tiles = sb("tiles", [DG, 2, 2], I32)
        trow = sb("trow", [1, NG, 2], I32)
        cnt = sb("cnt", [1, NG])
        one_row = sb("one_row", [1, NG])
        cum = sb("cum", [1, NG])
        tab = sb("tab", [1, 2 * NG, 3], I32)
        iota_n = sb("iota_n", [P, NP])
        ident = sb("ident", [P, P])
        tri = sb("tri", [P, P])
        ones = sb("ones", [P, P])
        zeros = sb("zeros", [P, P])
        wkv = sb("wkv", [P, 2, 2 * D])
        hsum = sb("hsum", [P, 2 * H2])
        w1t_s = sb("w1t_s", [P, 2, D])
        gw2_s = sb("gw2_s", [P, 2, D])
        wq_s = sb("wq_s", [P, 2, D])
        wo_s = sb("wo_s", [P, 2, D])
        w12 = sb("w12", [P, 2, D])
        kvT = sb("kvT", [P, 2, P])
        t1 = sb("t1", [P, 2, D])
        mixm = sb("mixm", [P, 2, D])
        kvg = sb("kvg", [P, 2 * D])
        kvb = sb("kvb", [P, 2 * D])
        bo_s = sb("bo_s", [P, D])
        gam = sb("gam", [P, D])
        bet = sb("bet", [P, D])
        gw = sb("gw", [P, 2, X])
        gb = sb("gb", [P, X])

        acc = sb("acc", [P, T * D])
        gath = [sb(f"gath{b}", [P, CG, D]) for b in range(GB)]
        gidx = [sb(f"gidx{b}", [P, CG], I32) for b in range(GB)]
        hot = [sb(f"hot{k}", [P, P]) for k in range(CG)]
        scr = sb("scr", [P, 64])
        scr_a = sb("scr_a", [P, 3])
        hot2 = [sb(f"osum{b}", [P, D])[:] for b in range(2)]

        xin = [sb(f"xin{b}", [P, D]) for b in range(2)]
        xno = [sb(f"xno{b}", [P, D]) for b in range(2)]
        xT = [sb(f"xT{b}", [P, 2, P]) for b in range(2)]
        yT = [sb(f"yT{b}", [P, 2, P]) for b in range(2)]
        res = [sb(f"res{b}", [P, D]) for b in range(2)]
        sq = sb("sq", [P, 2 * D])
        kvn = sb("kvn", [P, 2 * D])
        r8 = sb("r8", [P, 2, H2])
        st6 = sb("st6", [P, 6])
        mv = sb("mv", [P, 2])
        mva = sb("mva", [P, T, 2])
        sda = sb("sda", [P, T])
        rsa = sb("rsa", [P, T])

        def whole(b):
            return gath[b][:, :, :].rearrange("p c d -> p (c d)")
        we1 = [whole(b)[:, 0:2 * FF].rearrange("p (a f) -> p a f", a=2) for b in range(2)]
        we2 = [whole(b)[:, 2 * FF - 0:2 * FF + 4 * D].rearrange("p (a f) -> p a f", a=4) for b in range(2)]
        hT = [whole(2 + b)[:, 0:512].rearrange("p (a f) -> p a f", a=4) for b in range(2)]
        eo = [whole(2 + b)[:, 512:512 + D] for b in range(2)]
        be2 = [whole(2 + b)[:, 768:768 + D] for b in range(2)]
        ys = [whole(2 + b)[:, 1024:1024 + RW] for b in range(2)]
        be1 = [sb(f"be1{b}", [P, 4]) for b in range(2)]
        yk = [whole(b)[:, 0:2 * RW].rearrange("p (k w) -> p k w", k=2) for b in range(2)]
        FS = GB
        cy = [[whole(b)[:, n * D:(n + 1) * D] for n in range(6)] for b in range(FS)]
        blank = sb("blank", [P, RW])
        plc = sb("plc", [P, T, 2, 4])
        places = sb("places", [P, ST])
        eplc = [sb(f"eplc{b}", [P, 1], I32) for b in range(2)]
        pidx = [sb(f"pidx{b}", [P, 2], I32) for b in range(2)]

        n_r = T * X

        def rt(n, m=n_r):
            return acc[:, n * n_r:n * n_r + m]
        lg = sb("lg", [P, n_r])
        mx = [sb(f"mx{k}", [P, T]) for k in range(2)]
        ix = [sb(f"ix{k}", [P, T]) for k in range(2)]
        pw = [sb(f"pw{k}", [P, T]) for k in range(2)]
        pos = sb("pos", [P, T, 2], I32)
        posf = sb("posf", [P, T, 2])
        iota_x = sb("iota_x", [P, X])
        tok = sb("tok", [P, T, 4])
        crs = [sb(f"crs{b}", [P, 3]) for b in range(GB)]
        cmv = [sb(f"cmv{b}", [P, 2]) for b in range(GB)]
        nt_i = sb("nt_i", [P, X], I32)
        nt_f = sb("nt_f", [P, 3, X])
        eid = sb("eid", [1, ST], I32)

        s_wt = sem("s_wt"); s_pool = sem("s_pool"); s_pc = sem("s_pc"); s_dve = sem("s_dve")
        s_x = [sem(f"s_x{c}") for c in range(NC)]; s_xv = sem("s_xv"); s_xs = sem("s_xs")
        s_xn = sem("s_xn"); s_xst = sem("s_xst"); s_m_var = sem("s_m_var"); s_m_sd = sem("s_m_sd")
        s_sch = sem("s_sch"); s_sch_st = sem("s_sch_st"); s_sch_ld = sem("s_sch_ld"); s_tab = sem("s_tab")
        s_g = [sem(f"s_g{b}") for b in range(GB)]; s_gdone = sem("s_gdone")
        s_oh = [sem(f"s_oh{k}") for k in range(CG)]
        s_used = [sem(f"s_used{k}") for k in range(CG)]
        s_mm = sem("s_mm"); s_ev = sem("s_ev")
        s_acc = sem("s_acc"); s_h1 = sem("s_h1")
        s_m_ld = sem("s_m_ld"); s_m_tp = sem("s_m_tp"); s_m_xT = sem("s_m_xT"); s_m_mm = sem("s_m_mm")
        s_m_sq = sem("s_m_sq"); s_m_kvn = sem("s_m_kvn"); s_m_acc = sem("s_m_acc")
        s_b_out = sem("s_b_out"); s_b_st = sem("s_b_st")
        s_w = sem("s_w"); s_wc = sem("s_wc")
        s_d_o = sem("s_d_o"); s_d_tp = sem("s_d_tp"); s_d_oT = sem("s_d_oT"); s_d_mm = sem("s_d_mm")
        s_d_ld = [sem(f"s_d_ld{b}") for b in range(2)]; s_d_x1 = sem("s_d_x1"); s_d_y = sem("s_d_y")
        s_d_st = [sem(f"s_d_st{b}") for b in range(2)]
        s_d_yt = sem("s_d_yt"); s_d_yT = sem("s_d_yT"); s_d_lg = sem("s_d_lg"); s_d_lgc = sem("s_d_lgc")
        s_r_mask = sem("s_r_mask"); s_r_mm = sem("s_r_mm"); s_r_pos = sem("s_r_pos"); s_zero = sem("s_zero")
        s_zs = sem("s_zs"); s_exp = sem("s_exp"); s_x1_st = sem("s_x1_st")
        s_y_ld = [sem(f"s_y_ld{b}") for b in range(2)]; s_sc = [sem(f"s_sc{b}") for b in range(2)]; s_pi = sem("s_pi")
        s_e_w1 = [sem(f"s_e_w1{b}") for b in range(2)]; s_e_w2 = [sem(f"s_e_w2{b}") for b in range(2)]
        s_e_x = [sem(f"s_e_x{b}") for b in range(2)]; 
        s_e_tp = sem("s_e_tp"); s_e_yT = sem("s_e_yT"); s_eid = sem("s_eid"); s_pd = sem("s_pd")
        s_e_h = sem("s_e_h"); s_e_hT = sem("s_e_hT"); s_e_o = sem("s_e_o"); s_e_ev = sem("s_e_ev")
        s_e_st = [sem(f"s_e_st{b}") for b in range(2)]
        s_f_ld = [sem(f"s_f_ld{b}") for b in range(GB)]; s_f_xb = sem("s_f_xb"); s_f_ln = sem("s_f_ln")
        s_f_var = sem("s_f_var"); s_f_sd = sem("s_f_sd")
        s_f_out = sem("s_f_out"); s_f_st = [sem(f"s_f_st{b}") for b in range(GB)]

        def group_steps(eng, g):
            row = bass.ds(g, 1)
            return (eng.value_load(tab[0:1, row, 0], min_val=0, max_val=STEPS),
                    eng.value_load(tab[0:1, row, 1], min_val=1, max_val=STEPS),
                    eng.value_load(tab[0:1, row, 2], min_val=0, max_val=STEPS + T))

        def tile_of(step, shift):
            return nc.s_assert_within(step + shift - STEPS, 0, T - 1,
                                      skip_runtime_bounds_check_because="it is a tile number")

        def rows(t, i):
            return t[bass.ds(i * P, P), :]

        consts = [(srcs[:, 0:NCH], src_t), (srcs[:, NCH:NCH + GB * CG], src_t[:, 0:GB * CG]), (dsti[:], dst_t), (wts[:], wt_t),
                  (wkv[:], wkv_t.rearrange("(a p) n -> p a n", p=P)),
                  (w1t_s[:], w1t.rearrange("(a p) n -> p a n", p=P)),
                  (gw2_s[:], gw2.rearrange("(a p) n -> p a n", p=P)),
                  (wq_s[:], wq.rearrange("(a p) n -> p a n", p=P)),
                  (wo_s[:], wo_t.rearrange("(a p) n -> p a n", p=P)),
                  (kvg[:], kv_g.partition_broadcast(P)), (kvb[:], kv_b.partition_broadcast(P)),
                  (bo_s[:], bo.partition_broadcast(P)), (gam[:], gamma.partition_broadcast(P)),
                  (bet[:], beta.partition_broadcast(P)),
                  (gw[:], gate_w.rearrange("(a p) n -> p a n", p=P)),
                  (gb[:], gate_b.partition_broadcast(P))]
        CONST = 16 * len(consts)
        block = ctx.enter_context(nc.Block())

        @block.sync
        def _(sp):
            sp.dma_start(dgr[:], dst_g).then_inc(s_sch_ld, 16)

            def block_rows(t, c):
                return t[bass.ds(c * (CT * P), CT * P), :].rearrange("(q p) d -> p q d", p=P)

            def block_sb(c):
                return acc[:, bass.ds(c * (CT * D), CT * D)].rearrange("p (q d) -> p q d", d=D)

            for c in range(NC):
                sp.dma_start(block_sb(c), block_rows(x, c)).then_inc(s_x[c], 16)
            with sp.Fori(0, NC) as c:
                sp.wait_ge(s_xn, c + 1)
                sp.dma_start(block_rows(xn_d, c), block_sb(c)).then_inc(s_xst, 16)
            sp.wait_ge(s_sch, 1)
            sp.dma_start(sched_d.rearrange("(p c) m -> p c m", c=2), tiles[:]).then_inc(s_sch_st, 16)
            sp.wait_ge(s_sch_st, 16)
            sp.dma_start(trow[:], sched_d.rearrange("(o g) m -> o g m", o=1)).then_inc(s_sch_ld, 16)

            sp.wait_ge(s_zero, 2)
            for k in range(0, ST, 16):
                m = min(16, ST - k)
                sp.dma_start(ys_d[k * P:(k + m) * P, :].rearrange("(p r) w -> p r w", p=P),
                             blank[:].unsqueeze(1).broadcast_to([P, m, RW])).then_inc(s_zs, 16)
            sp.wait_ge(s_xst, 16 * NC)
            sp.dma_start(xno[0][:], rows(xn_d, 0)).then_inc(s_m_ld, 16)
            with sp.Fori(1, T) as i:
                sp.wait_ge(s_m_tp, i)
                sp.dma_start(xno[0][:], rows(xn_d, i)).then_inc(s_m_ld, 16)
            sp.wait_ge(s_acc, 1)
            sp.dma_start(h1_d.rearrange("(t p) d -> p t d", p=P),
                         acc[:].rearrange("p (t d) -> p t d", d=D)).then_inc(s_h1, 16)
            sp.wait_ge(s_m_tp, T)
            sp.dma_start(xno[0][:], rows(xn_d, 0)).then_inc(s_m_ld, 16)
            sp.dma_start(xin[0][:], rows(x, 0)).then_inc(s_m_ld, 16)
            with sp.Fori(1, T) as i:
                sp.wait_ge(s_m_tp, i + T)
                sp.dma_start(xno[0][:], rows(xn_d, i)).then_inc(s_m_ld, 16)
                sp.wait_ge(s_b_out, i)
                sp.dma_start(rows(base_d, i - 1), res[0][:]).then_inc(s_b_st, 16)
                sp.dma_start(xin[0][:], rows(x, i)).then_inc(s_m_ld, 16)
            sp.wait_ge(s_b_out, T)
            sp.dma_start(base_d[(T - 1) * P:NP, :], res[0][:]).then_inc(s_b_st, 16)
            sp.wait_ge(s_b_st, 16 * T)

            def d_load(i, b):
                sp.dma_start(xin[b][:], rows(base_d, i)).then_inc(s_d_ld[b], 16)

            d_load(0, 0)
            d_load(1, 1)
            with sp.Fori(0, T // 2) as j:
                for b in range(2):
                    sp.wait_ge(s_d_x1, j * 2 + b + 1)
                    d_load(j * 2 + 2 if b == 0 else (j * 2 + 3) % T, b)
            sp.wait_ge(s_d_x1, T)
            sp.dma_start(x1_d.rearrange("(t p) d -> p t d", p=P),
                         acc[:].rearrange("p (t d) -> p t d", d=D)).then_inc(s_x1_st, 16)
            with sp.Fori(0, T // 2) as j:
                for b in range(2):
                    sp.wait_ge(s_d_y, j * 2 + b + 1)
                    sp.dma_start(rows(y_d, j * 2 + b), xno[b][:]).then_inc(s_d_st[b], 16)
            sp.wait_ge(s_d_y, T)
            sp.dma_start(rows(y_d, T - 1), xno[0][:]).then_inc(s_d_st[0], 16)
            sp.wait_ge(s_d_ld[1], 16 * (T // 2 + 1))
            sp.wait_ge(s_d_st[0], 16 * (T // 2 + 1))
            sp.wait_ge(s_d_st[1], 16 * (T // 2))

            def y_load(i, b):
                for k in range(2):
                    sp.dma_start(yk[b][:, k, 0:D], rows(y_d, i)).then_inc(s_y_ld[b], 16)

            y_load(0, 0)
            y_load(1, 1)
            with sp.Fori(0, T // 2) as j:
                for b in range(2):
                    sp.wait_ge(s_sc[b], j * 32 + 32)
                    y_load(j * 2 + 2 if b == 0 else (j * 2 + 3) % T, b)
            sp.wait_ge(s_sc[0], 32 * (T // 2 + 1))
            sp.wait_ge(s_y_ld[1], 32 * (T // 2 + 1))
            sp.wait_ge(s_eid, 1)

            def expert(i):
                return sp.value_load(eid[0:1, bass.ds(i, 1)], min_val=0, max_val=X - 1)

            def x_load(i, b):
                sp.dma_start(ys[b], rows(ys_d, i)).then_inc(s_e_x[b], 16)

            def w1_load(e, b):
                sp.dma_start(we1[b], w1[bass.ds(e, 1), :, :].rearrange("o (a p) f -> p (o a) f", p=P)
                             ).then_inc(s_e_w1[b], 16)
                sp.dma_start(be1[b][:], b1_t[bass.ds(e, 1), :, :].rearrange("o p a -> p (o a)")
                             ).then_inc(s_e_w1[b], 16)

            def w2_load(e, b):
                sp.dma_start(we2[b], w2[bass.ds(e, 1), :, :].rearrange("o (a p) f -> p (o a) f", p=P)
                             ).then_inc(s_e_w2[b], 16)
                sp.dma_start(be2[b], b2[bass.ds(e, 1), :].rearrange("o d -> (o d)").partition_broadcast(P)
                             ).then_inc(s_e_w2[b], 16)

            for b in range(2):
                x_load(b, b)
                w1_load(expert(b), b)
            w2_load(expert(0), 0)

            def e_turn(i, b):
                last = isinstance(i, int) and i + 2 >= ST
                e2 = expert(i + 1)
                if not last:
                    e1 = expert(i + 2)
                    sp.wait_ge(s_e_yT, i + 1)
                    x_load(i + 2, b)
                    sp.wait_ge(s_e_hT, i + 1)
                    w1_load(e1, b)
                wait_from(sp, s_e_ev, i)
                w2_load(e2, 1 - b)

            e_turn(0, 0)
            e_turn(1, 1)
            with sp.Fori(1, ST // 2 - 1) as j:
                for b in range(2):
                    e_turn(j * 2 + b, b)
            e_turn(ST - 3, 0)
            e_turn(ST - 2, 1)

            sp.wait_ge(s_e_st[0], 16 * (ST // 2 + 1))
            sp.wait_ge(s_e_st[1], 16 * (ST // 2))

            ekn = eo_d.rearrange("(k n) d -> n k d", k=2)

            def f_load(i, b, n):
                wait_from(sp, s_f_out, i - (FS - 1))
                sp.dma_start(cy[b][0], rows(y_d, i)).then_inc(s_f_ld[b], 16)
                sp.dma_start(whole(b)[:, D:3 * D].rearrange("p (k d) -> p k d", k=2),
                             ekn[bass.ds(i * P, P), :, :]).then_inc(s_f_ld[b], 16)
                sp.dma_start(cy[b][3], rows(x1_d, i)).then_inc(s_f_ld[b], 16)
            in_turns(sp, T, FS, f_load)
            for b in range(FS):
                sp.wait_ge(s_f_st[b], 16 * len(range(b, T, FS)))

        @block.gpsimd
        def _(pool):
            pool.iota(iota_n[:], [[1, NP]], base=0, channel_multiplier=0,
                      allow_small_or_imprecise_dtypes=True).then_inc(s_pool, 1)
            pool.iota(tok[:], [[P, T], [0, 4]], base=0, channel_multiplier=1,
                      allow_small_or_imprecise_dtypes=True).then_inc(s_pool, 1)
            pool.memset(ident[:], 0.0).then_inc(s_pc, 1)
            pool.memset(tri[:], 0.0).then_inc(s_pc, 1)
            pool.memset(ones[:], 1.0).then_inc(s_pool, 1)
            pool.memset(blank[:, 0:D], 0.0).then_inc(s_zero, 1)
            pool.memset(blank[:, D:RW], float(NONE)).then_inc(s_zero, 1)
            pool.memset(zeros[:], 0.0).then_inc(s_pool, 1)
            pool.wait_ge(s_pc, 2)
            pool.affine_select(out=ident[:], in_=ident[:], compare_op=ALU.not_equal, fill=1.0, base=0,
                               pattern=[[-1, P]], channel_multiplier=1).then_inc(s_pool, 1)
            pool.affine_select(out=tri[:], in_=tri[:], compare_op=ALU.is_ge, fill=1.0, base=0,
                               pattern=[[-1, P]], channel_multiplier=1).then_inc(s_pool, 1)
            pool.wait_ge(s_wt, CONST)
            pool.wait_ge(s_xst, 16 * NC)
            for layer in range(2):
                if layer:
                    pool.wait_ge(s_h1, 16)
                table = xn_d if layer == 0 else h1_d
                with pool.Fori(0, NI) as i:
                    for b in range(GB):
                        g = i * GB + b
                        pool.wait_ge(s_gdone, g + 1 + NG * layer)
                        pool.nop(nofuse=True)
                        for k in range(CG):
                            pool.indirect_dma_start(gath[b][:, k, :], None, table,
                                                    bass.IndirectOffsetOnAxis(ap=gidx[b][:, k:k + 1], axis=0)
                                                    ).then_inc(s_g[b], 16)
            pool.wait_ge(s_r_pos, 1)
            pool.wait_ge(s_zs, 16 * -(-ST // 16))

            def scatter(i, b, n):
                pool.wait_ge(s_y_ld[b], n * 32 + 32)
                pool.tensor_copy(pidx[b][:], pos[:, bass.ds(i, 1), :].rearrange("p o k -> p (o k)")
                                 ).then_inc(s_pi, 1)
                pool.tensor_copy(yk[b][:, :, D:RW], plc[:, bass.ds(i, 1), :, :].rearrange("p o k w -> p (o k) w")
                                 ).then_inc(s_pi, 1)
                pool.wait_ge(s_pi, i * 2 + 2)
                pool.nop(nofuse=True)
                for k in range(2):
                    pool.indirect_dma_start(ys_d, bass.IndirectOffsetOnAxis(ap=pidx[b][:, k:k + 1], axis=0),
                                            yk[b][:, k, :], None).then_inc(s_sc[b], 16)

            with pool.Fori(0, T // 2) as j:
                for b in range(2):
                    scatter(j * 2 + b, b, j)
            scatter(T - 1, 0, T // 2)

            def e_scatter(i, b, n):
                pool.wait_ge(s_e_ev, i + 1)
                pool.nop(nofuse=True)
                pool.indirect_dma_start(eo_d, bass.IndirectOffsetOnAxis(ap=eplc[b][:], axis=0), eo[b], None,
                                        bounds_check=NONE - 1, oob_is_err=False).then_inc(s_e_st[b], 16)
            in_pairs(pool, ST, e_scatter)

            def c_tile(i, b, n):
                pool.wait_ge(s_f_ld[b], n * 48 + 48)
                pool.tensor_tensor(cy[b][4], cy[b][3], bet[:], ALU.add).then_inc(s_f_xb, 1)
                pool.wait_ge(s_f_xb, i + 1)
                wait_from(pool, s_f_st[b], n * 16)
                pool.wait_ge(s_f_ln, i + 1)
                pool.tensor_tensor(cy[b][5], cy[b][4], cy[b][2], ALU.add).then_inc(s_f_out, 1)
            in_turns(pool, T, FS, c_tile)

        @block.scalar
        def _(act):
            for dst, s in consts:
                act.dma_start(dst, s).then_inc(s_wt, 16)
            for c in range(NC):
                act.wait_ge(s_xv, c + 1)
                a = sda[:, c * CT:(c + 1) * CT]
                act.activation(a, a, ACT.Sqrt).then_inc(s_xs, 1)
            def sum_group(i, b, layer):
                before, after, shift = group_steps(act, i * GB + b + NG * layer)
                with act.Fori(before, after) as step:
                    t = tile_of(step, shift)
                    act.wait_ge(s_mm, step + 1)
                    act.activation(acc[:, bass.ds(t * D, D)], sums[:, bass.ds(step % 2 * 512, D)], ACT.Copy
                                   ).then_inc(s_ev, 1)
                act.wait_ge(s_gdone, i * GB + (b + GB + NG * layer))
                act.activation(gidx[b][:], srcs[:, bass.ds((i * GB + (b + GB)) * CG, CG)], ACT.Copy
                               ).then_inc(s_gdone, 1)

            def xn_turned(i, layer):
                act.wait_ge(s_m_tp, i + 1 + T * layer)
                if layer == 1:
                    act.wait_ge(s_m_mm, i + T)
                act.activation(xT[0][:], bank[1][:, 0:D].rearrange("p (a q) -> p a q", a=2), ACT.Copy
                               ).then_inc(s_m_xT, 1)

            def squares(i):
                act.wait_ge(s_m_mm, i + 1)
                act.activation(sq[:], bank[2][:], ACT.Square).then_inc(s_m_sq, 1)

            def roots(i):
                act.wait_ge(s_m_var, i + 1)
                act.activation(r8[:, 1, :], r8[:, 0, :], ACT.Sqrt).then_inc(s_m_sd, 1)

            act.wait_ge(s_pool, 6)
            act.wait_ge(s_wt, CONST)
            for b in range(GB):
                act.activation(gidx[b][:], srcs[:, b * CG:(b + 1) * CG], ACT.Copy).then_inc(s_gdone, 1)
            act.wait_ge(s_tab, 1)
            for layer in range(2):
                with act.Fori(0, NI) as i:
                    for b in range(GB):
                        sum_group(i, b, layer)
                        if b == 0:
                            xn_turned(i, layer)
                            if layer == 0:
                                squares(i)
                        if b == 1 and layer == 0:
                            roots(i)
                act.activation(scr_a[:, 1 + layer:2 + layer], ones[:, 0:1], ACT.Copy).then_inc(s_acc, 1)

            def take(i, b):
                wait_from(act, s_d_tp, i - 1)
                act.activation(hot2[b], acc[:, bass.ds(i * D, D)], ACT.Copy).then_inc(s_d_o, 1)

            def sums_tile(i, b, n):
                if not isinstance(i, int) or i < T - 1:
                    take(i + 1, 1 - b)
                act.wait_ge(s_d_tp, i + 1)
                wait_from(act, s_d_mm, i - 1)
                act.activation(xT[b][:], bank[b][:, 0:D].rearrange("p (a q) -> p a q", a=2), ACT.Copy
                               ).then_inc(s_d_oT, 1)

            def y_tile(i, b, n):
                act.wait_ge(s_d_yt, i + 1)
                wait_from(act, s_d_lg, i - 1)
                act.activation(yT[b][:], bank[4 + b][:, 0:D].rearrange("p (a q) -> p a q", a=2), ACT.Copy
                               ).then_inc(s_d_yT, 1)

            take(0, 0)
            in_pairs(act, T, sums_tile)
            act.wait_ge(s_xv, NC + 1)
            act.activation(sda[:], sda[:], ACT.Sqrt).then_inc(s_xs, 1)
            in_pairs(act, T, y_tile)
            act.wait_ge(s_pd, 1)
            act.activation(pw[1][:], pw[1][:], ACT.Exp).then_inc(s_exp, 1)

            def e_tile(i, b, n):
                if not isinstance(i, int) or i < ST - 1:
                    turned(i + 1, 1 - b)
                act.wait_ge(s_e_h, i + 1)
                wait_from(act, s_e_o, i - 1)
                for f in range(4):
                    ins = act.activation(hT[b][:, f, :], bank[2 + b][:, f * P:(f + 1) * P], ACT.Relu,
                                         bias=be1[b][:, f:f + 1])
                ins.then_inc(s_e_hT, 1)

            def turned(i, b):
                act.wait_ge(s_e_tp, i + 1)
                act.activation(places[:, bass.ds(i, 1)], ys[b][:, D:D + 1], ACT.Copy)
                act.activation(yT[b][:], bank[b][:, 0:D].rearrange("p (a q) -> p a q", a=2), ACT.Copy
                               ).then_inc(s_e_yT, 1)

            turned(0, 0)
            in_pairs(act, ST, e_tile)

            def root(i, b, n):
                act.wait_ge(s_f_var, i + 1)
                act.activation(crs[b][:, 1:2], crs[b][:, 0:1], ACT.Sqrt).then_inc(s_f_sd, 1)
                if not isinstance(i, int) or i > 0:
                    store(i - 1, (b - 1) % FS)

            def store(i, b):
                act.wait_ge(s_f_out, i + 1)
                act.dma_start(rows(out, i), cy[b][5]).then_inc(s_f_st[b], 16)
            in_turns(act, T, FS, root)
            store(T - 1, (T - 1) % FS)

        @block.tensor
        def _(pe):
            def transpose(ps, row_tile, signal):
                for a in range(2):
                    ins = pe.transpose(ps[:, a * P:(a + 1) * P], row_tile[:, a * P:(a + 1) * P], ident[:])
                ins.then_inc(signal, 1)

            pe.wait_ge(s_wt, CONST)
            pe.wait_ge(s_pool, 6)
            for i in range(2):
                for a in range(2):
                    ins = pe.matmul(bank[4 + i][:, 0:D], w1t_s[:, a, i * P:(i + 1) * P], gw2_s[:, a, :],
                                    start=a == 0, stop=a == 1)
            ins.then_inc(s_w, 1)
            for p in range(2):
                pe.matmul(bank[3][:, p * P:(p + 1) * P], zeros[:], zeros[:], start=p == 0, stop=False,
                          skip_group_check=True)
            pe.wait_ge(s_tab, 1)
            pe.wait_ge(s_wc, 1)

            def kv_proj(i):
                pe.wait_ge(s_m_ld, i * 16 + 16)
                transpose(bank[1], xno[0], s_m_tp)
                pe.wait_ge(s_m_xT, i + 1)
                for a in range(2):
                    ins = pe.matmul(bank[2][:], xT[0][:, a, :], wkv[:, a, :], start=a == 0, stop=a == 1)
                ins.then_inc(s_m_mm, 1)

            def kv_sum(i, m):
                pe.wait_ge(s_m_kvn, i + 1)
                for p in range(2):
                    ins = pe.matmul(bank[3][:, p * P:(p + 1) * P], kvn[0:m, D + p * P:D + (p + 1) * P],
                                    kvn[0:m, p * P:(p + 1) * P], start=False, stop=False, skip_group_check=True)
                ins.then_inc(s_m_acc, 1)

            def base_rows(i):
                pe.wait_ge(s_m_ld, i * 32 + (16 * T + 32))
                transpose(bank[1], xno[0], s_m_tp)
                pe.wait_ge(s_m_xT, i + 1 + T)
                wait_from(pe, s_b_out, i)
                for a in range(2):
                    ins = pe.matmul(bank[2][:, 0:D], xT[0][:, a, :], mixm[:, a, :], start=a == 0, stop=a == 1)
                ins.then_inc(s_m_mm, 1)

            def sum_group(i, b, layer):
                before, after, shift = group_steps(pe, i * GB + b + NG * layer)
                with pe.Fori(before, after) as step:
                    t = tile_of(step, shift)
                    out = sums[:, bass.ds(step % 2 * 512, D)]
                    pe.wait_ge(s_g[b], i * (16 * CG) + 16 * CG * (1 + NI * layer))
                    pe.wait_ge(s_ev, step + 1)
                    for k in range(CG):
                        pe.wait_ge(s_oh[k], step + 1)
                        pe.matmul(out, hot[k][:], gath[b][:, k, :], start=k == 0, stop=False
                                  ).then_inc(s_used[k], 1)
                    pe.wait_ge(s_ev, step + 2)
                    pe.matmul(out, ident[:], acc[:, bass.ds(t * D, D)], start=False, stop=True
                              ).then_inc(s_mm, 1)

            def edge_turn(i, layer, last):
                for b in range(GB):
                    sum_group(i, b, layer)
                    if b == 0:
                        if layer == 0:
                            kv_proj(i)
                        else:
                            base_rows(i)
                    if b == 3 and layer == 0:
                        kv_sum(i, N - (T - 1) * P if last else P)

            with pe.Fori(0, NI - 1) as i:
                edge_turn(i, 0, False)
            edge_turn(NI - 1, 0, True)
            pe.wait_ge(s_wc, 2)
            for p in range(2):
                ins = pe.matmul(bank[4 + p][:, 0:D], kvT[:, p, :], wo_s[:, p, :], start=True, stop=True)
            ins.then_inc(s_w, 1)
            pe.wait_ge(s_wc, 3)
            for i in range(2):
                for p in range(2):
                    ins = pe.matmul(bank[6 - 5 * i][:, 0:D], wq_s[:, p, i * P:(i + 1) * P], t1[:, p, :],
                                    start=p == 0, stop=p == 1)
            ins.then_inc(s_w, 1)
            pe.wait_ge(s_wc, 4)
            edge_turn(0, 1, False)
            with pe.Fori(1, NI) as i:
                edge_turn(i, 1, False)

            def sums_mm(i, b):
                pe.wait_ge(s_d_oT, i + 1)
                wait_from(pe, s_d_x1, i - 1)
                for a in range(2):
                    ins = pe.matmul(bank[2 + b][:, 0:D], xT[b][:, a, :], w12[:, a, :], start=a == 0, stop=a == 1)
                ins.then_inc(s_d_mm, 1)

            def sums_tile(i, b, n):
                pe.wait_ge(s_d_o, i + 1)
                transpose(bank[b], hot2[b], s_d_tp)
                if not isinstance(i, int) or i > 0:
                    sums_mm(i - 1, 1 - b)

            def gate_mm(i, b):
                pe.wait_ge(s_d_yT, i + 1)
                wait_from(pe, s_d_lgc, i - 1)
                for a in range(2):
                    ins = pe.matmul(bank[6 + b][:, 0:X], yT[b][:, a, :], gw[:, a, :], start=a == 0, stop=a == 1)
                ins.then_inc(s_d_lg, 1)

            def y_tile(i, b, n):
                pe.wait_ge(s_d_y, i + 1)
                transpose(bank[4 + b], xno[b], s_d_yt)
                if not isinstance(i, int) or i > 0:
                    gate_mm(i - 1, 1 - b)

            in_pairs(pe, T, sums_tile)
            sums_mm(T - 1, 0)
            in_pairs(pe, T, y_tile)
            gate_mm(T - 1, 0)
            pe.wait_ge(s_r_mask, 1)
            half = n_r // 2
            for h in range(2):
                pe.matmul(bank[h][:, 0:half], tri[:], rt(0)[:, h * half:(h + 1) * half], start=True, stop=True)
                ins = pe.matmul(bank[2 + h][:, 0:half], ones[:], rt(0)[:, h * half:(h + 1) * half],
                                start=True, stop=True)
            ins.then_inc(s_r_mm, 1)

            def turn_rows(i, b, n):
                pe.wait_ge(s_e_x[b], n * 16 + 16)
                transpose(bank[b], ys[b], s_e_tp)

            def out_mm(i, b, n):
                pe.wait_ge(s_e_w2[b], n * 32 + 32)
                pe.wait_ge(s_e_hT, i + 1)
                wait_from(pe, s_e_ev, i - 1)
                for f in range(4):
                    ins = pe.matmul(bank[4 + b][:, 0:D], hT[b][:, f, :], we2[b][:, f, :], start=f == 0,
                                    stop=f == 3)
                ins.then_inc(s_e_o, 1)

            def e_tile(i, b, n):
                if not isinstance(i, int) or i < ST - 1:
                    turn_rows(i + 1, 1 - b, n + b)
                pe.wait_ge(s_e_w1[b], n * 32 + 32)
                pe.wait_ge(s_e_yT, i + 1)
                for f in range(4):
                    for a in range(2):
                        ins = pe.matmul(bank[2 + b][:, f * P:(f + 1) * P], we1[b][:, a, f * P:(f + 1) * P],
                                        yT[b][:, a, :], start=a == 0, stop=a == 1)
                ins.then_inc(s_e_h, 1)
                if not isinstance(i, int) or i > 0:
                    out_mm(i - 1, 1 - b, n + b - 1)

            turn_rows(0, 0, 0)
            in_pairs(pe, ST, e_tile)
            out_mm(ST - 1, 0, ST // 2)

        @block.vector
        def _(dve):
            own = Links(dve, s_dve)
            link = own.link

            marks = iter(range(64))

            def mark(signal):
                c = next(marks)
                dve.memset(scr[:, c:c + 1], 0.0).then_inc(signal, 1)

            def stats(t, src):
                link(dve.bn_stats(st6[:], src))
                dve.nop(nofuse=True)
                link(dve.bn_aggr(mv[:], st6[:]))
                link(dve.tensor_copy(mva[:, t, :] if isinstance(t, int) else
                                     mva[:, bass.ds(t, 1), :].rearrange("p o m -> p (o m)"), mv[:]))

            def col(a, t):
                return a[:, t:t + 1] if isinstance(t, int) else a[:, bass.ds(t, 1)]

            def mean(t):
                return mva[:, t, 0:1] if isinstance(t, int) else mva[:, bass.ds(t, 1), 0]

            def normed(dst, src, t):
                return dve.tensor_scalar(dst, src, mean(t), col(rsa, t), ALU.subtract, ALU.mult)

            def deviations(t0, n, ready, rooted, at):
                dve.tensor_scalar(sda[:, t0:t0 + n], mva[:, t0:t0 + n, 1], EPS, None, ALU.add).then_inc(ready, 1)
                dve.wait_ge(rooted, at)
                link(dve.reciprocal(rsa[:, t0:t0 + n], sda[:, t0:t0 + n]))

            dve.wait_ge(s_sch_ld, 16)
            link(dve.tensor_reduce(mnmx[:, :, 0], dgr[:], AX.X, ALU.min))
            link(dve.tensor_reduce(mnmx[:, :, 1], dgr[:], AX.X, ALU.max))
            dve.tensor_scalar(tiles[:], mnmx[:], 7, None, ALU.arith_shift_right).then_inc(s_sch, 1)

            for c in range(NC):
                dve.wait_ge(s_x[c], 16)
                for q in range(CT):
                    t = c * CT + q
                    stats(t, acc[:, t * D:(t + 1) * D])
                deviations(c * CT, CT, s_xv, s_xs, c + 1)
                for q in range(CT):
                    t = c * CT + q
                    a = acc[:, t * D:(t + 1) * D]
                    link(normed(a, a, t))
                mark(s_xn)

            dve.wait_ge(s_wt, CONST)
            link(dve.tensor_copy(dstf[:], dsti[:]))
            wv = wkv[:].rearrange("p a (h c) -> p (a h) c", c=HD)
            link(dve.tensor_reduce(hsum[:], wv, AX.X, ALU.add))
            link(dve.tensor_scalar(hsum[:], hsum[:], 1.0 / HD, None, ALU.mult))
            link(dve.tensor_tensor(wv, wv, hsum[:].unsqueeze(2).broadcast_to([P, 2 * H2, HD]), ALU.subtract))
            dve.wait_ge(s_w, 1)
            for i in range(2):
                link(dve.tensor_copy(w12[:, i, :], bank[4 + i][:, 0:D]))
            link(dve.memset(one_row[:], 1.0))
            dve.wait_ge(s_sch_ld, 32)
            tb = tab[:].rearrange("o (l g) m -> o l g m", l=2)
            link(dve.tensor_tensor(cnt[:], trow[:, :, 1], trow[:, :, 0], ALU.subtract))
            link(dve.tensor_scalar(cnt[:], cnt[:], 1.0, None, ALU.add))
            link(dve.tensor_tensor_scan(cum[:], one_row[:], cnt[:], 0.0, ALU.mult, ALU.add))
            link(dve.tensor_copy(tb[:, 0, :, 1], cum[:]))
            link(dve.tensor_tensor(tb[:, 0, :, 0], cum[:], cnt[:], ALU.subtract))
            for c in range(2):
                link(dve.tensor_scalar(tb[:, 1, :, c], tb[:, 0, :, c], cum[:, NG - 1:NG], None, ALU.add))
            for l in range(2):
                link(dve.tensor_tensor(tb[:, l, :, 2], trow[:, :, 0], tb[:, l, :, 0], ALU.subtract))
            for l in range(2):
                link(dve.tensor_scalar(tb[:, l, :, 2], tb[:, l, :, 2], float(STEPS), None, ALU.add))
            mark(s_tab)
            dve.wait_ge(s_tab, 1)
            link(dve.memset(kvT[:], 0.0))
            dve.wait_ge(s_xst, 16 * NC)
            link(dve.memset(acc[:], 0.0))
            for k in range(2):
                mark(s_ev)
            for k in range(CG):
                dve.memset(hot[k][:, 0:1], 0.0).then_inc(s_used[k], 1)
            mark(s_wc)
            dve.wait_ge(s_pool, 6)
            dve.wait_ge(s_wc, 1)

            def hot_group(i, b, layer):
                g = i * GB + b
                before, after, shift = group_steps(dve, g + NG * layer)
                with dve.Fori(before, after) as step:
                    t = tile_of(step, shift)
                    for k in range(CG):
                        c = g * CG + k
                        dve.wait_ge(s_used[k], step + 1)
                        dve.tensor_scalar(hot[k][:], iota_n[:, bass.ds(t * P, P)], dstf[:, bass.ds(c, 1)],
                                          wts[:, bass.ds(c, 1)], ALU.is_equal, ALU.mult).then_inc(s_oh[k], 1)

            def kv_vars(i):
                dve.wait_ge(s_m_sq, i + 1)
                link(dve.tensor_reduce(r8[:, 0, :], sq[:].rearrange("p (h c) -> p h c", c=HD), AX.X, ALU.add))
                dve.tensor_scalar(r8[:, 0, :], r8[:, 0, :], 1.0 / HD, EPS, ALU.mult, ALU.add).then_inc(s_m_var, 1)

            def kv_norm(i):
                dve.wait_ge(s_m_sd, i + 1)
                link(dve.reciprocal(r8[:, 1, :], r8[:, 1, :]))
                wait_from(dve, s_m_acc, i)
                link(dve.tensor_tensor(kvn[:].rearrange("p (h c) -> p h c", c=HD),
                                       bank[2][:].rearrange("p (h c) -> p h c", c=HD),
                                       r8[:, 1, :].unsqueeze(2).broadcast_to([P, H2, HD]), ALU.mult))
                link(dve.tensor_tensor(kvn[:], kvn[:], kvg[:], ALU.mult))
                dve.tensor_tensor(kvn[:], kvn[:], kvb[:], ALU.add).then_inc(s_m_kvn, 1)

            def base_add(i):
                dve.wait_ge(s_m_mm, i + (1 + T))
                dve.wait_ge(s_m_ld, i * 32 + (16 * T + 32))
                if not isinstance(i, int):
                    dve.wait_ge(s_b_st, i * 16)
                link(dve.tensor_tensor(res[0][:], bank[2][:, 0:D], xin[0][:], ALU.add))
                dve.tensor_tensor(res[0][:], res[0][:], bo_s[:], ALU.add).then_inc(s_b_out, 1)

            def edge_turn(i, layer):
                for b in range(GB):
                    hot_group(i, b, layer)
                    if layer == 0 and b == 1:
                        kv_vars(i)
                    if layer == 0 and b == 2:
                        kv_norm(i)
                    if layer == 1 and b == 1:
                        base_add(i)

            edge_turn(0, 0)
            own.enter()
            with dve.Fori(1, NI) as i:
                own.turn(i - 1, 4)
                edge_turn(i, 0)
            own.leave(NI - 1, 4)
            dve.wait_ge(s_m_acc, T)
            for h in range(4):
                p, o = h // 2, (h % 2) * HD
                link(dve.tensor_scalar(kvT[o:o + HD, p, o:o + HD], bank[3][o:o + HD, p * P + o:p * P + o + HD],
                                       1.0 / N, None, ALU.mult))
            mark(s_wc)
            dve.wait_ge(s_w, 2)
            for p in range(2):
                link(dve.tensor_copy(t1[:, p, :], bank[4 + p][:, 0:D]))
            mark(s_wc)
            dve.wait_ge(s_w, 3)
            for p in range(2):
                link(dve.tensor_copy(mixm[:, p, :], bank[6 - 5 * p][:, 0:D]))
            dve.wait_ge(s_h1, 16)
            link(dve.memset(acc[:], 0.0))
            mark(s_wc)
            edge_turn(0, 1)
            own.enter()
            with dve.Fori(1, NI) as i:
                own.turn(i - 1, 1)
                edge_turn(i, 1)
            own.leave(NI - 1, 1)
            dve.wait_ge(s_gdone, GB + 2 * NG)

            dve.wait_ge(s_b_st, 16 * T)

            def x1_tile(i, b, n):
                dve.wait_ge(s_d_mm, i + 1)
                dve.wait_ge(s_d_ld[b], n * 16 + 16)
                link(dve.tensor_tensor(res[b][:], bank[2 + b][:, 0:D], xin[b][:], ALU.add))
                dve.tensor_copy(acc[:, bass.ds(i * D, D)], res[b][:]).then_inc(s_d_x1, 1)
                stats(i, res[b][:])

            own.enter()
            with dve.Fori(0, T // 2) as j:
                own.turn(j, 8)
                for b in range(2):
                    x1_tile(j * 2 + b, b, j)
            own.leave(T // 2, 8)
            x1_tile(T - 1, 0, T // 2)
            deviations(0, T, s_xv, s_xs, NC + 1)

            def y_tile(i, b):
                wait_from(dve, s_d_yt, i - 1)
                normed(xno[b][:], acc[:, bass.ds(i * D, D)], i).then_inc(s_d_y, 1)

            def logits(i, b):
                dve.wait_ge(s_d_lg, i + 1)
                dve.tensor_tensor(lg[:, bass.ds(i * X, X)], bank[6 + b][:, 0:X], gb[:], ALU.add
                                  ).then_inc(s_d_lgc, 1)

            for b in range(2):
                y_tile(b, b)
            with dve.Fori(1, T // 2) as j:
                for b in range(2):
                    dve.wait_ge(s_d_st[b], j * 16)
                    y_tile(j * 2 + b, b)
                    logits(j * 2 + b - 2, b)
            dve.wait_ge(s_d_st[0], 16 * (T // 2))
            y_tile(T - 1, 0)
            for i in range(T - 3, T):
                logits(i, i % 2)
            dve.wait_ge(s_x1_st, 16)
            dve.wait_ge(s_d_lgc, T)

            def v3(ap):
                return ap.rearrange("p (t e) -> p t e", e=X)

            def per_t(ap):
                return ap.unsqueeze(2).broadcast_to([P, T, X])

            def per_e(ap):
                return ap.unsqueeze(1).broadcast_to([P, T, X])

            link(dve.tensor_copy(iota_x[:], iota_n[:, 0:X]))
            cur = lg[:]
            for k in range(2):
                link(dve.tensor_reduce(mx[k][:], v3(cur), AX.X, ALU.max))
                link(dve.tensor_tensor(v3(rt(1)), v3(cur), per_t(mx[k][:]), ALU.not_equal))
                link(dve.tensor_scalar(rt(1), rt(1), float(X), None, ALU.mult))
                link(dve.tensor_tensor(v3(rt(1)), v3(rt(1)), per_e(iota_x[:]), ALU.add))
                link(dve.tensor_reduce(ix[k][:], v3(rt(1)), AX.X, ALU.min))
                link(dve.tensor_tensor(v3(rt(2 + k)), per_e(iota_x[:]), per_t(ix[k][:]), ALU.is_equal))
                if k == 0:
                    link(dve.tensor_scalar(rt(4), rt(2), -3.0e38, None, ALU.mult))
                    link(dve.tensor_scalar(rt(5), rt(2), -1.0, 1.0, ALU.mult, ALU.add))
                    link(dve.tensor_tensor(rt(5), rt(5), lg[:], ALU.mult))
                    link(dve.tensor_tensor(rt(6), rt(4), rt(5), ALU.add))
                    cur = rt(6)
            dve.tensor_tensor(rt(0), rt(2), rt(3), ALU.add).then_inc(s_r_mask, 1)
            dve.wait_ge(s_r_mm, 1)
            half = n_r // 2
            for h in range(2):
                link(dve.tensor_copy(rt(7)[:, h * half:(h + 1) * half], bank[2 + h][:, 0:half]))
                link(dve.tensor_copy(rt(8)[:, h * half:(h + 1) * half], bank[h][:, 0:half]))
            tot_e = rt(9).rearrange("p (e t) -> p e t", t=T)
            link(dve.tensor_copy(tot_e, rt(7).rearrange("p (t e) -> p e t", e=X)))
            link(dve.memset(rt(10), 1.0))
            link(dve.memset(rt(10).rearrange("p (e t) -> p e t", t=T)[:, :, 0], 0.0))
            link(dve.tensor_tensor_scan(rt(11), rt(10), rt(9), 0.0, ALU.mult, ALU.add))
            run_e = rt(11).rearrange("p (e t) -> p e t", t=T)
            link(dve.tensor_scalar(nt_i[:], run_e[:, :, T - 1], float(P - 1), None, ALU.add))
            link(dve.tensor_scalar(nt_i[:], nt_i[:], 7, None, ALU.arith_shift_right))
            link(dve.tensor_copy(nt_f[:, 0, :], nt_i[:]))
            link(dve.tensor_tensor_scan(nt_f[:, 1, :], ones[:, 0:X], nt_f[:, 0, :], 0.0, ALU.mult, ALU.add))
            link(dve.tensor_tensor(nt_f[:, 2, :], nt_f[:, 1, :], nt_f[:, 0, :], ALU.subtract))
            link(dve.tensor_tensor(rt(11), rt(11), rt(9), ALU.subtract))
            link(dve.tensor_tensor(v3(rt(8)), v3(rt(8)), rt(11).rearrange("p (e t) -> p t e", t=T), ALU.add))
            link(dve.tensor_scalar(nt_f[:, 2, :], nt_f[:, 2, :], float(P), None, ALU.mult))
            link(dve.tensor_tensor(v3(rt(8)), v3(rt(8)), per_e(nt_f[:, 2, :]), ALU.add))
            for k in range(2):
                link(dve.tensor_tensor(rt(1), rt(8), rt(2 + k), ALU.mult))
                link(dve.tensor_reduce(posf[:, :, k], v3(rt(1)), AX.X, ALU.add))
            link(dve.tensor_copy(pos[:], posf[:]))
            for k in range(2):
                link(dve.tensor_scalar(plc[:, :, k, :], tok[:], float(k * NP), None, ALU.add))
            mark(s_r_pos)
            sel = acc[0:1, 0:ST * X].rearrange("o (i e) -> o i e", e=X)
            link(dve.tensor_tensor(sel, iota_n[0:1, 0:ST].unsqueeze(2).broadcast_to([1, ST, X]),
                                   nt_f[0:1, 1, :].unsqueeze(1).broadcast_to([1, ST, X]), ALU.is_ge))
            link(dve.tensor_reduce(cnt[:, 0:ST], sel, AX.X, ALU.add))
            dve.tensor_scalar(eid[:], cnt[:, 0:ST], float(X - 1), None, ALU.min).then_inc(s_eid, 1)
            dve.tensor_tensor(pw[1][:], mx[1][:], mx[0][:], ALU.subtract).then_inc(s_pd, 1)
            dve.wait_ge(s_exp, 1)
            link(dve.tensor_scalar(pw[0][:], pw[1][:], 1.0, None, ALU.add))
            link(dve.reciprocal(pw[0][:], pw[0][:]))
            link(dve.tensor_tensor(pw[1][:], pw[1][:], pw[0][:], ALU.mult))

            def e_tile(i, b, n):
                wait_from(dve, s_e_st[b], n * 16)
                dve.wait_ge(s_e_yT, i + 1)
                dve.tensor_copy(eplc[b][:], places[:, bass.ds(i, 1)])
                dve.wait_ge(s_e_o, i + 1)
                dve.tensor_tensor(eo[b], bank[4 + b][:, 0:D], be2[b], ALU.add).then_inc(s_e_ev, 1)

            in_pairs(dve, ST, e_tile)

            def c_tile(i, b, n):
                first = not isinstance(i, int) or i < T
                second = not isinstance(i, int) or i > 0
                p = (b - 1) % FS
                c, q = cy[b], cy[p]
                if first:
                    dve.wait_ge(s_f_ld[b], n * 48 + 48)
                    own.post(dve.scalar_tensor_tensor(out=c[0], in0=c[1], scalar=col(pw[0], i), in1=c[0],
                                                      op0=ALU.mult, op1=ALU.add))
                if second:
                    dve.wait_ge(s_f_sd, i)
                    own.post(dve.reciprocal(crs[p][:, 2:3], crs[p][:, 1:2]))
                if first:
                    own.until(1 if second else 0)
                    own.post(dve.scalar_tensor_tensor(out=c[0], in0=c[2], scalar=col(pw[1], i), in1=c[0],
                                                      op0=ALU.mult, op1=ALU.add))
                if second:
                    own.until(1 if first else 0)
                    own.post(dve.tensor_scalar(q[1], q[0], cmv[p][:, 0:1], crs[p][:, 2:3],
                                               ALU.subtract, ALU.mult))
                if first:
                    own.until(1 if second else 0)
                    own.post(dve.bn_stats(st6[:], c[0]))
                if second:
                    own.until(1 if first else 0)
                    dve.tensor_tensor(q[2], q[1], gam[:], ALU.mult).then_inc(s_f_ln, 1)
                if first:
                    own.until(0)
                    dve.nop(nofuse=True)
                    link(dve.bn_aggr(cmv[b][:], st6[:]))
                    dve.tensor_scalar(crs[b][:, 0:1], cmv[b][:, 1:2], EPS, None, ALU.add).then_inc(s_f_var, 1)

            for i in range(FS):
                c_tile(i, i, 0)
            own.enter()
            with dve.Fori(1, T // FS) as j:
                own.turn(j - 1, 6 * FS)
                for b in range(FS):
                    c_tile(j * FS + b, b, j)
            own.leave(T // FS - 1, 6 * FS)
            for i in range(T // FS * FS, T + 1):
                c_tile(i, i % FS, i // FS)


def kernel(**inputs):
    import numpy as np
    import concourse.bacc as bacc
    from concourse.bass_utils import run_bass_kernel_spmd as run

    def pad(a, value):
        return np.concatenate([np.asarray(a), np.full((EP - E,), value, np.asarray(a).dtype)])

    def columns(a):
        return np.ascontiguousarray(a.reshape(NCH, P).T)

    f = {k: np.asarray(v) for k, v in inputs.items()}
    dst = pad(f["dst"], N - 1)
    arrays = {
        "x": np.concatenate([f["x"], np.zeros((NP - N, D), np.float32)]),
        "src_t": columns(pad(f["src"], 0)),
        "dst_t": columns(dst),
        "dst_g": dst.reshape(DG, 2, P * CG),
        "wt_t": columns(pad(f["edge_weight"], 0)),
        "w1t": f["L0_gnn_W1"].T,
        "gw2": f["L0_gnn_W2"],
        "wq": f["L0_mix_wq"],
        "wkv_t": np.concatenate([f["L0_mix_wk"], f["L0_mix_wv"]]).T,
        "wo_t": f["L0_mix_wo"].T,
        "bo": f["L0_mix_bo"],
        "kv_g": np.concatenate([f["L0_mix_ln_k_g"]] * 4 + [f["L0_mix_ln_v_g"]] * 4),
        "kv_b": np.concatenate([f["L0_mix_ln_k_b"]] * 4 + [f["L0_mix_ln_v_b"]] * 4),
        "gate_w": f["L0_ffn_gate_w"],
        "gate_b": f["L0_ffn_gate_b"],
        "w1": f["L0_ffn_w1"],
        "b1_t": f["L0_ffn_b1"].reshape(X, FF // P, P).transpose(0, 2, 1),
        "w2": f["L0_ffn_w2"],
        "b2": f["L0_ffn_b2"],
        "gamma": f["L0_ffn_gamma"],
        "beta": f["L0_ffn_beta"],
    }
    nc = bacc.Bacc("TRN2", target_bir_lowering=False, num_devices=1)
    given, args = {}, []
    for name, a in arrays.items():
        a = np.ascontiguousarray(a)
        given[f"in_{name}"] = a
        args.append(nc.dram_tensor(f"in_{name}", a.shape, mybir.dt.from_np(a.dtype), kind="ExternalInput").ap())
    args.append(nc.dram_tensor("out_rows", (NP, D), F32, kind="ExternalOutput").ap())
    gps_layer(nc, *args)
    r = run(nc, [given], core_ids=[0])
    return r.results[0]["out_rows"][:N]
```

```python
from contextlib import ExitStack

import concourse.bass as bass
from concourse import mybir

F32 = mybir.dt.float32
I32 = mybir.dt.int32
U32 = mybir.dt.uint32
ALU = mybir.AluOpType
ACT = mybir.ActivationFunctionType
AX = mybir.AxisListType

P = 128
N = 6250
D = 256
E = 200000
T = -(-N // P)
NP = T * P
HD = 64
H2 = 2 * D // HD
CG = 8
GB = 4
NG = -(-E // (P * CG * GB)) * GB
NCH = NG * CG
EP = NCH * P
NI = NG // GB
X = 16
FF = 512
ST = (2 * NP) // P + X - 1
NO_SLOT = 1 << 20
RW = D + 4
NONE = 2 * NP
EPS = 1e-5
REG = NP + P
STEPS = 2 * NG * T
CT = 7
NC = T // CT
assert NC * CT == T
assert NI == T and T % 2 == 1 and ST % 2 == 1
DG = NG // 2


class Links:

    def __init__(self, eng, sem):
        self.eng, self.sem, self.at, self.n = eng, sem, 0, 0

    def link(self, ins):
        ins.then_inc(self.sem, 1)
        self.n += 1
        self.eng.wait_ge(self.sem, self.at + self.n)

    def post(self, ins):
        ins.then_inc(self.sem, 1)
        self.n += 1

    def until(self, back):
        self.eng.wait_ge(self.sem, self.at + (self.n - back))

    def turn(self, i, per):
        self.at = self.base + i * per
        self.n = 0

    def enter(self):
        self.base = self.at + self.n

    def leave(self, turns, per):
        assert self.n == per, self.n
        self.at, self.n = self.base + turns * per, 0


class Parts:

    def __init__(self, eng, sem, per):
        self.eng, self.sem, self.per = eng, sem, per

    def start(self, u, b):
        self.at = u * sum(self.per) + sum(self.per[:b])
        self.n = 0

    def link(self, ins):
        ins.then_inc(self.sem, 1)
        self.n += 1
        self.eng.wait_ge(self.sem, self.at + self.n)


def in_pairs(eng, half, tile):
    for b in range(2):
        tile(b, b, 0, False)
    with eng.Fori(1, half) as j:
        for b in range(2):
            tile(j * 2 + b, b, j, False)
    tile(half * 2, 0, half, True)


def in_turns(eng, n, slots, tile):
    for b in range(slots):
        tile(b, b, 0)
    with eng.Fori(1, n // slots) as j:
        for b in range(slots):
            tile(j * slots + b, b, j)
    for i in range(n // slots * slots, n):
        tile(i, i % slots, i // slots)


def wait_from(eng, sem, value):
    if not isinstance(value, int) or value > 0:
        eng.wait_ge(sem, value)


def gps_layer(nc, x, src_t, dst_t, dst_g, wt_t, w1t, gw2, wq, wkv_t, wo_t, bo, kv_g, kv_b,
              gate_w, gate_b, w1, b1_t, w2, b2, gamma, beta, out):
    with ExitStack() as ctx:
        def sb(name, shape, dt=F32):
            return ctx.enter_context(nc.sbuf_tensor(name, shape, dt))

        def sem(name):
            return ctx.enter_context(nc.semaphore(name))

        def dram(name, shape, dt=F32):
            return nc.dram_tensor(name, shape, dt, kind="Internal").ap()

        sums = ctx.enter_context(nc.psum_tensor("sums", [P, 1024], F32))
        bank = [ctx.enter_context(nc.psum_tensor(f"bank{n}", [P, 512], F32)) for n in range(1, 7)]
        bank = [sums[:, 0:512]] + [t[:] for t in bank] + [sums[:, 512:1024]]

        xn_d = dram("xn_d", [NP, D])
        h1_d = dram("h1_d", [NP, D])
        y_d = dram("y_d", [NP, D])
        sched_d = dram("sched_d", [NG, 2], I32)
        ys_d = dram("ys_d", [X * REG + (X - 1) * P, RW])
        eo_d = dram("eo_d", [2 * NP, D])

        srcs = sb("srcs", [P, NCH + GB * CG], I32)
        dsti = sb("dsti", [P, NCH], I32)
        dstf = sb("dstf", [P, NCH])
        wts = sb("wts", [P, NCH])
        dgr = sb("dgr", [DG, 2, P * CG], I32)
        mnmx = sb("mnmx", [DG, 2, 2], I32)
        tiles = sb("tiles", [DG, 2, 2], I32)
        trow = sb("trow", [1, NG, 2], I32)
        cnt = sb("cnt", [1, NG])
        one_row = sb("one_row", [1, NG])
        cum = sb("cum", [1, NG])
        tab = sb("tab", [1, 2 * NG, 3], I32)
        tmin = [sb(f"tmin{k}", [1, T + 64]) for k in range(2)]
        fin = sb("fin", [1, T + 1])
        has = sb("has", [1, T])
        made_i = sb("made_i", [1, T + 3], I32)
        iota_n = sb("iota_n", [P, NP])
        ident = sb("ident", [P, P])
        tri = sb("tri", [P, P])
        ones = sb("ones", [P, P])
        zeros = sb("zeros", [P, P])
        wkv = sb("wkv", [P, 2, 2 * D])
        hsum = sb("hsum", [P, 2 * H2])
        w1t_s = sb("w1t_s", [P, 2, D])
        gw2_s = sb("gw2_s", [P, 2, D])
        wq_s = sb("wq_s", [P, 2, D])
        wo_s = sb("wo_s", [P, 2, D])
        w12 = sb("w12", [P, 2, D])
        kvT = sb("kvT", [P, 2, P])
        t1 = sb("t1", [P, 2, D])
        mixm = sb("mixm", [P, 2, D])
        kvg = sb("kvg", [P, 2 * D])
        kvb = sb("kvb", [P, 2 * D])
        bo_s = sb("bo_s", [P, D])
        gam = sb("gam", [P, D])
        bet = sb("bet", [P, D])
        gw = sb("gw", [P, 2, X])
        gb = sb("gb", [P, X])

        acc = sb("acc", [P, T * D])
        gath = [sb(f"gath{b}", [P, CG, D]) for b in range(GB)]
        gidx = [sb(f"gidx{b}", [P, CG], I32) for b in range(GB)]
        hot = [sb(f"hot{k}", [P, P]) for k in range(CG)]
        scr = sb("scr", [P, 64])
        scr_p = sb("scr_p", [P, 1])
        scr_a = sb("scr_a", [P, 3])
        nsum = sb("nsum", [P, D])

        xin = sb("xin", [P, D])
        xno = sb("xno", [P, D])
        xT = sb("xT", [P, 2, P])
        yT = [sb(f"yT{b}", [P, 2, P]) for b in range(2)]
        sq = sb("sq", [P, 2 * D])
        kvn = sb("kvn", [P, 2 * D])
        r8 = sb("r8", [P, 2, H2])
        st6 = sb("st6", [P, 6])
        st_b = sb("st_b", [P, CT, 6])
        mv = sb("mv", [P, 2])
        mva = sb("mva", [P, T, 2])
        sda = sb("sda", [P, T])
        rsa = sb("rsa", [P, T])

        def whole(b):
            return gath[b][:, :, :].rearrange("p c d -> p (c d)")
        we1 = [whole(b)[:, 0:2 * FF].rearrange("p (a f) -> p a f", a=2) for b in range(2)]
        we2 = [whole(b)[:, 2 * FF:2 * FF + 4 * D].rearrange("p (a f) -> p a f", a=4) for b in range(2)]
        hT = [whole(2 + b)[:, 0:512].rearrange("p (a f) -> p a f", a=4) for b in range(2)]
        eo = [whole(2 + b)[:, 512:512 + D] for b in range(2)]
        be2 = [whole(2 + b)[:, 768:768 + D] for b in range(2)]
        ys = [whole(2 + b)[:, 1024:1024 + RW] for b in range(2)]
        be1 = [sb(f"be1{b}", [P, 4]) for b in range(2)]
        yk = sb("yk", [P, 2, RW])
        yr = sb("yr", [P, D])
        FS = 2 * GB
        cr = [whole(b // 2)[:, b % 2 * 4 * D:(b % 2 + 1) * 4 * D] for b in range(FS)]
        cy = [[cr[b][:, n * D:(n + 1) * D] for n in range(4)] for b in range(FS)]
        blank = sb("blank", [P, RW])
        plc = sb("plc", [P, T, 2])
        places = sb("places", [P, ST])
        eplc = [sb(f"eplc{b}", [P, 1], I32) for b in range(2)]
        pidx = sb("pidx", [P, 2], I32)
        x1s = sb("x1s", [P, D])
        xs = sb("xs", [P, D])
        xT4 = sb("xT4", [P, 4, P])
        rs = sb("rs", [P, 3])
        lg = sb("lg", [P, 2, X])
        ne = sb("ne", [P, X])
        ohx = sb("ohx", [P, 2, X])
        mask = sb("mask", [P, X])
        msum = sb("msum", [P, X])
        rank = sb("rank", [P, X])
        prod = sb("prod", [P, 2, X])
        tmx = sb("tmx", [P, 2])
        tix = sb("tix", [P, 2])
        posf = sb("posf", [P, 2])
        mxa = sb("mxa", [P, T, 2])
        pw = [sb(f"pw{k}", [P, T]) for k in range(2)]
        iota_x = sb("iota_x", [P, X])
        eoff = sb("eoff", [P, X])
        tok = sb("tok", [P, T])
        crs = [sb(f"crs{b}", [P, 4]) for b in range(FS)]
        cmv = [sb(f"cmv{b}", [P, 2]) for b in range(FS)]
        nt_i = sb("nt_i", [P, X], I32)
        nt_f = sb("nt_f", [P, 2, X])
        eid = sb("eid", [1, ST], I32)
        erow = sb("erow", [1, ST], I32)
        pairs = sb("pairs", [1, 1], I32)
        ends = sb("ends", [1, X], I32)
        eraw = sb("eraw", [1, 2, ST])
        tcol = sb("tcol", [P, 3])

        s_wt = sem("s_wt"); s_pool = sem("s_pool"); s_pc = sem("s_pc"); s_dve = sem("s_dve")
        s_dve_x = sem("s_dve_x"); s_dve_p = sem("s_dve_p"); s_r_none = sem("s_r_none")
        s_x = [sem(f"s_x{c}") for c in range(NC)]; s_xv = sem("s_xv"); s_xs = sem("s_xs")
        s_xn = sem("s_xn"); s_xst = sem("s_xst"); s_m_var = sem("s_m_var"); s_m_sd = sem("s_m_sd")
        s_sch = sem("s_sch"); s_sch_st = sem("s_sch_st"); s_sch_ld = sem("s_sch_ld"); s_tab = sem("s_tab")
        s_g = [sem(f"s_g{b}") for b in range(GB)]; s_gdone = sem("s_gdone")
        s_oh = [sem(f"s_oh{k}") for k in range(CG)]
        s_used = [sem(f"s_used{k}") for k in range(CG)]
        s_mm = sem("s_mm"); s_ev = sem("s_ev")
        s_acc = sem("s_acc"); s_h1 = sem("s_h1")
        s_m_ld = sem("s_m_ld"); s_m_tp = sem("s_m_tp"); s_m_xT = sem("s_m_xT"); s_m_mm = sem("s_m_mm")
        s_m_sq = sem("s_m_sq"); s_m_kvn = sem("s_m_kvn"); s_m_acc = sem("s_m_acc")
        s_w = sem("s_w"); s_wc = sem("s_wc")
        s_d_o = sem("s_d_o"); s_d_tp = sem("s_d_tp"); s_d_oT = sem("s_d_oT"); s_d_mm = sem("s_d_mm")
        s_d_xn = sem("s_d_xn"); s_d_x = sem("s_d_x"); s_d_x1 = sem("s_d_x1"); s_kept = sem("s_kept"); s_d_xb = sem("s_d_xb"); s_ends = sem("s_ends")
        s_d_var = sem("s_d_var"); s_d_sd = sem("s_d_sd"); s_d_y = sem("s_d_y"); s_d_yk = sem("s_d_yk")
        s_d_yst = sem("s_d_yst"); s_d_yt = sem("s_d_yt"); s_d_yT = sem("s_d_yT"); s_d_lg = sem("s_d_lg")
        s_r_mask = sem("s_r_mask"); s_r_mm = sem("s_r_mm"); s_r_turn = sem("s_r_turn"); s_sc = sem("s_sc")
        s_r_all = sem("s_r_all"); s_zero = sem("s_zero"); s_zs = sem("s_zs"); s_exp = sem("s_exp")
        s_e_w1 = [sem(f"s_e_w1{b}") for b in range(2)]; s_e_w2 = [sem(f"s_e_w2{b}") for b in range(2)]
        s_e_x = [sem(f"s_e_x{b}") for b in range(2)]
        s_e_tp = sem("s_e_tp"); s_e_yT = sem("s_e_yT"); s_eid = sem("s_eid"); s_pd = sem("s_pd")
        s_e_h = sem("s_e_h"); s_e_hT = sem("s_e_hT"); s_e_o = sem("s_e_o"); s_e_ev = sem("s_e_ev")
        s_e_st = [sem(f"s_e_st{b}") for b in range(2)]
        s_f_ld = [sem(f"s_f_ld{b}") for b in range(FS)]; s_f_xb = sem("s_f_xb"); s_f_ln = sem("s_f_ln")
        s_f_var = sem("s_f_var"); s_f_r = sem("s_f_r"); s_f_sd = sem("s_f_sd")
        s_f_out = sem("s_f_out"); s_f_st = [sem(f"s_f_st{b}") for b in range(FS)]

        def group_steps(eng, g, before=None):
            row = bass.ds(g, 1)
            if before is None:
                before = eng.value_load(tab[0:1, row, 0], min_val=0, max_val=STEPS)
            return (before,
                    eng.value_load(tab[0:1, row, 1], min_val=1, max_val=STEPS),
                    eng.value_load(tab[0:1, row, 2], min_val=0, max_val=STEPS + T))

        def made(eng, i):
            return eng.value_load(made_i[0:1, bass.ds(i, 1)] if not isinstance(i, int) else made_i[0:1, i:i + 1],
                                  min_val=0, max_val=2 * T)

        def left_of(eng):
            return eng.value_load(made_i[0:1, T + 1:T + 2], min_val=0, max_val=T)

        def later(eng):
            return eng.value_load(made_i[0:1, T + 2:T + 3], min_val=0, max_val=NI)

        def u_tile(u):
            return nc.s_assert_within(u, 0, T - 1, skip_runtime_bounds_check_because="it is a tile number")

        def turn_of(u, more):
            return nc.s_assert_within(u + more, NI, NI + T,
                                      skip_runtime_bounds_check_because="u is at least the first tile left")

        def tile_of(step, shift):
            return nc.s_assert_within(step + shift - STEPS, 0, T - 1,
                                      skip_runtime_bounds_check_because="it is a tile number")

        def rows(t, i):
            return t[bass.ds(i * P, P), :]

        consts = [(srcs[:, 0:NCH], src_t), (srcs[:, NCH:NCH + GB * CG], src_t[:, 0:GB * CG]), (dsti[:], dst_t), (wts[:], wt_t),
                  (wkv[:], wkv_t.rearrange("(a p) n -> p a n", p=P)),
                  (w1t_s[:], w1t.rearrange("(a p) n -> p a n", p=P)),
                  (gw2_s[:], gw2.rearrange("(a p) n -> p a n", p=P)),
                  (wq_s[:], wq.rearrange("(a p) n -> p a n", p=P)),
                  (wo_s[:], wo_t.rearrange("(a p) n -> p a n", p=P)),
                  (kvg[:], kv_g.partition_broadcast(P)), (kvb[:], kv_b.partition_broadcast(P)),
                  (bo_s[:], bo.partition_broadcast(P)), (gam[:], gamma.partition_broadcast(P)),
                  (bet[:], beta.partition_broadcast(P)),
                  (gw[:], gate_w.rearrange("(a p) n -> p a n", p=P)),
                  (gb[:], gate_b.partition_broadcast(P))]
        CONST = 16 * len(consts)

        def tails(eng, half):
            for e in range(half, X, 2):
                end = eng.value_load(ends[0:1, e:e + 1], min_val=e * REG, max_val=e * REG + NP)
                eng.dma_start(ys_d[bass.ds(end, P), :], blank[:]).then_inc(s_zs, 16)

        def half_of(eng):
            return eng.value_load(pairs[0:1, 0:1], min_val=NP // P - 1, max_val=ST // 2 - 1) + 1

        def expert(eng, i):
            return eng.value_load(eid[0:1, i:i + 1] if isinstance(i, int) else eid[0:1, bass.ds(i, 1)],
                                  min_val=0, max_val=X)

        def new_expert(eng, e, ready, load):
            eng.nop(nofuse=True)
            with eng.If(e < X):
                load(nc.s_assert_within(e, 0, X - 1, skip_runtime_bounds_check_because="just compared"))
            with eng.Else():
                eng.sem_inc(ready, 32)

        def w1_load(eng, e, b):
            def load(e):
                eng.dma_start(we1[b], w1[bass.ds(e, 1), :, :].rearrange("o (a p) f -> p (o a) f", p=P)
                              ).then_inc(s_e_w1[b], 16)
                eng.dma_start(be1[b][:], b1_t[bass.ds(e, 1), :, :].rearrange("o p a -> p (o a)")
                              ).then_inc(s_e_w1[b], 16)
            new_expert(eng, e, s_e_w1[b], load)

        def w2_load(eng, e, b):
            def load(e):
                eng.dma_start(we2[b], w2[bass.ds(e, 1), :, :].rearrange("o (a p) f -> p (o a) f", p=P)
                              ).then_inc(s_e_w2[b], 16)
                eng.dma_start(be2[b], b2[bass.ds(e, 1), :].rearrange("o d -> (o d)").partition_broadcast(P)
                              ).then_inc(s_e_w2[b], 16)
            new_expert(eng, e, s_e_w2[b], load)

        block = ctx.enter_context(nc.Block())

        @block.sync
        def _(sp):
            sp.dma_start(dgr[:], dst_g).then_inc(s_sch_ld, 16)

            def block_rows(t, c):
                return t[bass.ds(c * (CT * P), CT * P), :].rearrange("(q p) d -> p q d", p=P)

            def block_sb(c):
                return acc[:, bass.ds(c * (CT * D), CT * D)].rearrange("p (q d) -> p q d", d=D)

            for c in range(NC):
                sp.dma_start(block_sb(c), block_rows(x, c)).then_inc(s_x[c], 16)
            with sp.Fori(0, NC) as c:
                sp.wait_ge(s_xn, c + 1)
                sp.dma_start(block_rows(xn_d, c), block_sb(c)).then_inc(s_xst, 16)
            sp.wait_ge(s_sch, 1)
            sp.dma_start(sched_d.rearrange("(p c) m -> p c m", c=2), tiles[:]).then_inc(s_sch_st, 16)
            sp.wait_ge(s_sch_st, 16)
            sp.dma_start(trow[:], sched_d.rearrange("(o g) m -> o g m", o=1)).then_inc(s_sch_ld, 16)

            sp.wait_ge(s_zero, 2)
            sp.dma_start(ys_d[X * REG:X * REG + (X - 1) * P, :].rearrange("(p r) w -> p r w", p=P),
                         blank[:].unsqueeze(1).broadcast_to([P, X - 1, RW])).then_inc(s_zs, 16)
            sp.wait_ge(s_xst, 16 * NC)
            sp.dma_start(xno[:], rows(xn_d, 0)).then_inc(s_m_ld, 16)
            sp.wait_ge(s_tab, 1)
            with sp.Fori(1, T) as i:
                u = made(sp, i + 1)
                sp.wait_ge(s_m_tp, i)
                sp.dma_start(xno[:], rows(xn_d, i)).then_inc(s_m_ld, 16)
                sp.wait_ge(s_gdone, i * GB + GB)
                sp.nop(nofuse=True)
                with sp.If(u < T):
                    sp.dma_start(rows(h1_d, u_tile(u)), acc[:, bass.ds(u_tile(u) * D, D)]).then_inc(s_h1, 16)
            sp.wait_ge(s_acc, 1)
            left = left_of(sp)
            with sp.If(left < T):
                with sp.Fori(left, T) as u:
                    sp.dma_start(rows(h1_d, u_tile(u)), acc[:, bass.ds(u_tile(u) * D, D)]).then_inc(s_h1, 16)
            sp.wait_ge(s_m_tp, T)
            sp.dma_start(xno[:], rows(xn_d, 0)).then_inc(s_d_xn, 16)
            sp.dma_start(xin[:], rows(x, 0)).then_inc(s_d_x, 16)
            with sp.Fori(0, T - 1) as u:
                sp.wait_ge(s_d_tp, u + 1)
                sp.dma_start(xno[:], rows(xn_d, u + 1)).then_inc(s_d_xn, 16)
                sp.wait_ge(s_d_x1, u + 1)
                sp.dma_start(xin[:], rows(x, u + 1)).then_inc(s_d_x, 16)
                sp.wait_ge(s_d_y, u + 1)
                sp.dma_start(rows(y_d, u), yr[:]).then_inc(s_d_yst, 16)
            sp.wait_ge(s_d_y, T)
            sp.dma_start(y_d[(T - 1) * P:NP, :], yr[:]).then_inc(s_d_yst, 16)
            sp.wait_ge(s_ends, 1)
            tails(sp, 0)
            sp.wait_ge(s_eid, 1)
            half = half_of(sp)
            for b in range(2):
                w1_load(sp, expert(sp, b), b)
            sp.wait_ge(s_d_yst, 16 * T + 16)
            sp.wait_ge(s_r_all, 1)
            sp.wait_ge(s_zs, 16 * (1 + X))

            def slot_row(i):
                return sp.value_load(erow[0:1, bass.ds(i, 1)], min_val=0, max_val=X * REG + (X - 2) * P)

            def x_load(row, b):
                sp.dma_start(ys[b], ys_d[bass.ds(row, P), :]).then_inc(s_e_x[b], 16)

            for b in range(2):
                x_load(slot_row(b), b)

            def e_turn(i, b, n, last):
                e = expert(sp, i + 2)
                row = slot_row(i + 2)
                sp.wait_ge(s_e_yT, i + 1)
                x_load(row, b)
                sp.wait_ge(s_e_h, i + 1)
                sp.wait_ge(s_e_hT, i + 1)
                w1_load(sp, e, b)

            in_pairs(sp, half - 1, e_turn)

            sp.wait_ge(s_e_st[0], half * 16 + 16)
            sp.wait_ge(s_e_st[1], half * 16)
            sp.nop(nofuse=True)

            ekn = eo_d.rearrange("(k n) d -> n k d", k=2)

            def f_load(i, b, n):
                wait_from(sp, s_f_out, i - (FS - 1))
                sp.dma_start(cy[b][0], rows(y_d, i)).then_inc(s_f_ld[b], 16)
                sp.dma_start(cr[b][:, D:3 * D].rearrange("p (k d) -> p k d", k=2),
                             ekn[bass.ds(i * P, P), :, :]).then_inc(s_f_ld[b], 16)
            in_turns(sp, T, FS, f_load)
            for b in range(FS):
                sp.wait_ge(s_f_st[b], 16 * len(range(b, T, FS)))

        @block.gpsimd
        def _(pool):
            pool.iota(iota_n[:], [[1, NP]], base=0, channel_multiplier=0,
                      allow_small_or_imprecise_dtypes=True).then_inc(s_pool, 1)
            pool.iota(tok[:], [[P, T]], base=0, channel_multiplier=1,
                      allow_small_or_imprecise_dtypes=True).then_inc(s_pool, 1)
            pool.memset(ident[:], 0.0).then_inc(s_pc, 1)
            pool.memset(tri[:], 0.0).then_inc(s_pc, 1)
            pool.memset(ones[:], 1.0).then_inc(s_pool, 1)
            pool.memset(blank[:, 0:D], 0.0).then_inc(s_zero, 1)
            pool.memset(blank[:, D:RW], float(NONE)).then_inc(s_zero, 1)
            pool.memset(zeros[:], 0.0).then_inc(s_pool, 1)
            pool.wait_ge(s_pc, 2)
            pool.affine_select(out=ident[:], in_=ident[:], compare_op=ALU.not_equal, fill=1.0, base=0,
                               pattern=[[-1, P]], channel_multiplier=1).then_inc(s_pool, 1)
            pool.affine_select(out=tri[:], in_=tri[:], compare_op=ALU.is_ge, fill=1.0, base=0,
                               pattern=[[-1, P]], channel_multiplier=1).then_inc(s_pool, 1)
            pool.wait_ge(s_wt, CONST)
            pool.wait_ge(s_xst, 16 * NC)

            def gathers(i, b, layer):
                pool.wait_ge(s_gdone, i * GB + (b + 1 + NG * layer))
                pool.nop(nofuse=True)
                for k in range(CG):
                    pool.indirect_dma_start(gath[b][:, k, :], None, h1_d if layer else xn_d,
                                            bass.IndirectOffsetOnAxis(ap=gidx[b][:, k:k + 1], axis=0)
                                            ).then_inc(s_g[b], 16)

            def scatter(n):
                pool.wait_ge(s_r_turn, n)
                pool.nop(nofuse=True)
                for k in range(2):
                    pool.indirect_dma_start(ys_d, bass.IndirectOffsetOnAxis(ap=pidx[:, k:k + 1], axis=0),
                                            yk[:, k, :], None, bounds_check=X * REG - 1, oob_is_err=False
                                            ).then_inc(s_sc, 16)

            with pool.Fori(0, NI) as i:
                for b in range(GB):
                    gathers(i, b, 0)
            pool.wait_ge(s_h1, 16 * T)
            for b in range(GB):
                gathers(0, b, 1)
            with pool.Fori(1, NI) as i:
                for b in range(GB):
                    gathers(i, b, 1)
                    if b == 1:
                        scatter(i)
            left, more = left_of(pool), later(pool)
            scatter(NI)
            scatter(NI + 1)
            with pool.If(left < T):
                with pool.Fori(left, T) as u:
                    scatter(turn_of(u, more) + 2)
            pool.wait_ge(s_sc, turn_of(T, more) * 32 + 32)
            pool.nop(nofuse=True)
            pool.memset(scr_p[:], 0.0).then_inc(s_r_all, 1)

            def e_scatter(i, b, n, last):
                pool.wait_ge(s_e_ev, i + 1)
                pool.nop(nofuse=True)
                pool.indirect_dma_start(eo_d, bass.IndirectOffsetOnAxis(ap=eplc[b][:], axis=0), eo[b], None,
                                        bounds_check=NONE - 1, oob_is_err=False).then_inc(s_e_st[b], 16)
            pool.wait_ge(s_eid, 1)
            in_pairs(pool, half_of(pool), e_scatter)

            def c_tile(i, b, n):
                pool.wait_ge(s_f_ln, i + 1)
                pool.tensor_tensor(cy[b][2], cy[b][1], gam[:], ALU.mult).then_inc(s_f_xb, 1)
                pool.wait_ge(s_f_xb, i + 1)
                wait_from(pool, s_f_st[b], n * 16)
                pool.nop(nofuse=True)
                pool.tensor_tensor(cy[b][3], cy[b][2], acc[:, bass.ds(i * D, D)], ALU.add).then_inc(s_f_out, 1)
            in_turns(pool, T, FS, c_tile)

        @block.scalar
        def _(act):
            for dst, s in consts:
                act.dma_start(dst, s).then_inc(s_wt, 16)
            for c in range(NC):
                act.wait_ge(s_xv, c + 1)
                a = sda[:, c * CT:(c + 1) * CT]
                act.activation(a, a, ACT.Sqrt).then_inc(s_xs, 1)
            def sum_group(i, b, layer, before):
                before, after, shift = group_steps(act, i * GB + b + NG * layer, before)
                with act.Fori(before, after) as step:
                    t = tile_of(step, shift)
                    act.wait_ge(s_mm, step + 1)
                    act.activation(acc[:, bass.ds(t * D, D)], sums[:, bass.ds(step % 2 * 512, D)], ACT.Copy
                                   ).then_inc(s_ev, 1)
                act.wait_ge(s_gdone, i * GB + (b + GB + NG * layer))
                act.activation(gidx[b][:], srcs[:, bass.ds((i * GB + (b + GB)) * CG, CG)], ACT.Copy
                               ).then_inc(s_gdone, 1)
                return after

            def xn_turned(i):
                act.wait_ge(s_m_tp, i + 1)
                act.activation(xT[:], bank[1][:, 0:D].rearrange("p (a q) -> p a q", a=2), ACT.Copy
                               ).then_inc(s_m_xT, 1)

            def squares(i):
                act.wait_ge(s_m_mm, i + 1)
                act.activation(sq[:], bank[2][:], ACT.Square).then_inc(s_m_sq, 1)

            def roots(i):
                act.wait_ge(s_m_var, i + 1)
                act.activation(r8[:, 1, :], r8[:, 0, :], ACT.Sqrt).then_inc(s_m_sd, 1)

            act.wait_ge(s_pool, 6)
            act.wait_ge(s_wt, CONST)
            for b in range(GB):
                act.activation(gidx[b][:], srcs[:, b * CG:(b + 1) * CG], ACT.Copy).then_inc(s_gdone, 1)
            act.wait_ge(s_tab, 1)
            with act.Fori(0, NI) as i:
                before = None
                for b in range(GB):
                    before = sum_group(i, b, 0, before)
                    if b == 0:
                        xn_turned(i)
                        squares(i)
                    if b == 1:
                        roots(i)
            act.activation(scr_a[:, 1:2], ones[:, 0:1], ACT.Copy).then_inc(s_acc, 1)

            def take(u):
                act.activation(nsum[:], acc[:, bass.ds(u * D, D)], ACT.Copy).then_inc(s_d_o, 1)

            def evict(u):
                act.wait_ge(s_d_tp, u + 1)
                act.activation(xT4[:], bank[1][:].rearrange("p (a q) -> p a q", a=4), ACT.Copy
                               ).then_inc(s_d_oT, 1)

            def root(u):
                act.wait_ge(s_d_var, u + 1)
                act.activation(rs[:, 1:2], rs[:, 0:1], ACT.Sqrt).then_inc(s_d_sd, 1)

            def keep(u):
                act.wait_ge(s_d_xb, u + 1)
                act.nop(nofuse=True)
                act.activation(acc[:, bass.ds(u * D, D)], xs[:], ACT.Copy)

            def evict_y(u):
                act.wait_ge(s_d_yt, u + 1)
                act.activation(yT[0][:], bank[3][:, 0:D].rearrange("p (a q) -> p a q", a=2), ACT.Copy
                               ).then_inc(s_d_yT, 1)

            def to_scatter(u, n):
                wait_from(act, s_sc, n * 32)
                act.wait_ge(s_d_y, u + 1)
                for k in range(2):
                    act.activation(yk[:, k, 0:D], yr[:], ACT.Copy)
                act.activation(yk[:, :, D:D + 1].rearrange("p k o -> p (k o)"),
                               plc[:, bass.ds(u, 1), :].rearrange("p o k -> p (o k)"), ACT.Copy
                               ).then_inc(s_d_yk, 1)

            act.activation(scr_a[:, 2:3], ones[:, 0:1], ACT.Copy).then_inc(s_kept, 1)
            with act.Fori(0, NI) as i:
                v, u = made(act, i), made(act, i + 1)
                act.wait_ge(s_gdone, i * GB + (GB + NG))
                act.nop(nofuse=True)
                with act.If(u < T):
                    take(u_tile(u))
                before = None
                for b in range(GB):
                    before = sum_group(i, b, 1, before)
                    if b == 0:
                        with act.If(u < T):
                            evict(u_tile(u))
                    if b == 2:
                        with act.If(v < T):
                            to_scatter(u_tile(v), i)
                        with act.If(u < T):
                            root(u_tile(u))
                    if b == 3:
                        act.wait_ge(s_gdone, i * GB + (2 * GB + NG))
                        act.nop(nofuse=True)
                        with act.If(u < T):
                            keep(u_tile(u))
                        act.activation(scr_a[:, 2:3], ones[:, 0:1], ACT.Copy).then_inc(s_kept, 1)
                        with act.If(u < T):
                            evict_y(u_tile(u))
            v, left, more = made(act, NI), left_of(act), later(act)
            with act.If(v < T):
                to_scatter(u_tile(v), NI)
            act.wait_ge(s_gdone, GB + 2 * NG)
            with act.If(left < T):
                with act.Fori(left, T) as u:
                    take(u_tile(u))
                    evict(u_tile(u))
                    root(u_tile(u))
                    keep(u_tile(u))
                    evict_y(u_tile(u))
                    to_scatter(u_tile(u), turn_of(u, more) + 1)
            act.wait_ge(s_ends, 1)
            tails(act, 1)
            act.wait_ge(s_pd, 1)
            act.activation(pw[1][:], pw[1][:], ACT.Exp).then_inc(s_exp, 1)

            def e_tile(i, b, n, last):
                if not last:
                    turned(i + 1, 1 - b)
                act.wait_ge(s_e_h, i + 1)
                wait_from(act, s_e_o, i - 1)
                for f in range(4):
                    ins = act.activation(hT[b][:, f, :], bank[2 + b][:, f * P:(f + 1) * P], ACT.Relu,
                                         bias=be1[b][:, f:f + 1])
                ins.then_inc(s_e_hT, 1)
                if not last:
                    e = expert(act, i + 1)
                    wait_from(act, s_e_ev, i)
                    w2_load(act, e, 1 - b)

            def turned(i, b):
                act.wait_ge(s_e_tp, i + 1)
                act.activation(places[:, bass.ds(i, 1)], ys[b][:, D:D + 1], ACT.Copy)
                act.activation(yT[b][:], bank[b][:, 0:D].rearrange("p (a q) -> p a q", a=2), ACT.Copy
                               ).then_inc(s_e_yT, 1)

            act.wait_ge(s_eid, 1)
            half = half_of(act)
            w2_load(act, expert(act, 0), 0)
            turned(0, 0)
            in_pairs(act, half, e_tile)

            def root(i, b, n):
                act.wait_ge(s_f_var, i + 1)
                act.activation(crs[b][:, 1:2], crs[b][:, 0:1], ACT.Sqrt).then_inc(s_f_sd, 1)
                if not isinstance(i, int) or i > 0:
                    norm(i - 1, (b - 1) % FS)
                if not isinstance(i, int) or i > 1:
                    store(i - 2, (b - 2) % FS)

            def norm(i, b):
                act.wait_ge(s_f_r, i + 1)
                act.activation(cy[b][1], cy[b][0], ACT.Identity, bias=crs[b][:, 3:4], scale=crs[b][:, 2:3]
                               ).then_inc(s_f_ln, 1)

            def store(i, b):
                act.wait_ge(s_f_out, i + 1)
                act.dma_start(rows(out, i), cy[b][3]).then_inc(s_f_st[b], 16)
            in_turns(act, T, FS, root)
            norm(T - 1, (T - 1) % FS)
            store(T - 2, (T - 2) % FS)
            store(T - 1, (T - 1) % FS)

        @block.tensor
        def _(pe):
            def transpose(ps, row_tile, signal):
                for a in range(2):
                    ins = pe.transpose(ps[:, a * P:(a + 1) * P], row_tile[:, a * P:(a + 1) * P], ident[:])
                ins.then_inc(signal, 1)

            pe.wait_ge(s_wt, CONST)
            pe.wait_ge(s_pool, 6)
            for i in range(2):
                for a in range(2):
                    ins = pe.matmul(bank[4 + i][:, 0:D], w1t_s[:, a, i * P:(i + 1) * P], gw2_s[:, a, :],
                                    start=a == 0, stop=a == 1)
            ins.then_inc(s_w, 1)
            for p in range(2):
                pe.matmul(bank[3][:, p * P:(p + 1) * P], zeros[:], zeros[:], start=p == 0, stop=False,
                          skip_group_check=True)
            pe.wait_ge(s_tab, 1)
            pe.wait_ge(s_wc, 1)

            def kv_proj(i):
                pe.wait_ge(s_m_ld, i * 16 + 16)
                transpose(bank[1], xno, s_m_tp)
                pe.wait_ge(s_m_xT, i + 1)
                for a in range(2):
                    ins = pe.matmul(bank[2][:], xT[:, a, :], wkv[:, a, :], start=a == 0, stop=a == 1)
                ins.then_inc(s_m_mm, 1)

            def kv_sum(i, m):
                pe.wait_ge(s_m_kvn, i + 1)
                for p in range(2):
                    ins = pe.matmul(bank[3][:, p * P:(p + 1) * P], kvn[0:m, D + p * P:D + (p + 1) * P],
                                    kvn[0:m, p * P:(p + 1) * P], start=False, stop=False, skip_group_check=True)
                ins.then_inc(s_m_acc, 1)

            def sum_group(i, b, layer, before):
                before, after, shift = group_steps(pe, i * GB + b + NG * layer, before)
                if layer == 1 and b == 0:
                    pe.wait_ge(s_kept, i + 1)
                    pe.nop(nofuse=True)
                with pe.Fori(before, after) as step:
                    t = tile_of(step, shift)
                    out = sums[:, bass.ds(step % 2 * 512, D)]
                    pe.wait_ge(s_g[b], i * (16 * CG) + 16 * CG * (1 + NI * layer))
                    pe.wait_ge(s_ev, step + 1)
                    for k in range(CG):
                        pe.wait_ge(s_oh[k], step + 1)
                        pe.matmul(out, hot[k][:], gath[b][:, k, :], start=k == 0, stop=False
                                  ).then_inc(s_used[k], 1)
                    pe.wait_ge(s_ev, step + 2)
                    pe.matmul(out, ident[:], acc[:, bass.ds(t * D, D)], start=False, stop=True
                              ).then_inc(s_mm, 1)
                return after

            def edge_turn(i, last):
                before = None
                for b in range(GB):
                    before = sum_group(i, b, 0, before)
                    if b == 0:
                        kv_proj(i)
                    if b == 3:
                        kv_sum(i, N - (T - 1) * P if last else P)

            with pe.Fori(0, NI - 1) as i:
                edge_turn(i, False)
            edge_turn(NI - 1, True)
            pe.wait_ge(s_wc, 2)
            for p in range(2):
                ins = pe.matmul(bank[4 + p][:, 0:D], kvT[:, p, :], wo_s[:, p, :], start=True, stop=True)
            ins.then_inc(s_w, 1)
            pe.wait_ge(s_wc, 3)
            for i in range(2):
                for p in range(2):
                    ins = pe.matmul(bank[6 - 5 * i][:, 0:D], wq_s[:, p, i * P:(i + 1) * P], t1[:, p, :],
                                    start=p == 0, stop=p == 1)
            ins.then_inc(s_w, 1)
            pe.wait_ge(s_wc, 4)

            def turn_in(u):
                pe.wait_ge(s_d_o, u + 1)
                pe.wait_ge(s_d_xn, u * 16 + 16)
                for a in range(2):
                    pe.transpose(bank[1][:, a * P:(a + 1) * P], nsum[:, a * P:(a + 1) * P], ident[:])
                transpose(bank[1][:, D:2 * D], xno, s_d_tp)

            def x1_mm(u):
                pe.wait_ge(s_d_oT, u + 1)
                for a in range(2):
                    pe.matmul(bank[2][:, 0:D], xT4[:, a, :], w12[:, a, :], start=a == 0, stop=False)
                for a in range(2):
                    ins = pe.matmul(bank[2][:, 0:D], xT4[:, 2 + a, :], mixm[:, a, :], start=False, stop=a == 1)
                ins.then_inc(s_d_mm, 1)

            def turn_y(u):
                pe.wait_ge(s_d_y, u + 1)
                transpose(bank[3], yr, s_d_yt)

            def gate_mm(u):
                pe.wait_ge(s_d_yT, u + 1)
                for a in range(2):
                    ins = pe.matmul(bank[4][:, 0:X], yT[0][:, a, :], gw[:, a, :], start=a == 0, stop=a == 1)
                ins.then_inc(s_d_lg, 1)

            def rank_mm(u):
                pe.wait_ge(s_r_mask, u + 1)
                pe.matmul(bank[5][:, 0:X], tri[:], mask[:], start=True, stop=False)
                pe.matmul(bank[5][:, 0:X], ones[:], msum[:], start=False, stop=True).then_inc(s_r_mm, 1)

            with pe.Fori(0, NI) as i:
                before = None
                for b in range(GB):
                    before = sum_group(i, b, 1, before)
                    if b == 0:
                        v, u = made(pe, i), made(pe, i + 1)
                        with pe.If(u < T):
                            turn_in(u_tile(u))
                        with pe.If(v < T):
                            gate_mm(u_tile(v))
                    if b == 1:
                        with pe.If(u < T):
                            x1_mm(u_tile(u))
                        with pe.If(v < T):
                            rank_mm(u_tile(v))
                    if b == 3:
                        with pe.If(u < T):
                            turn_y(u_tile(u))
            v, left = made(pe, NI), left_of(pe)
            with pe.If(v < T):
                gate_mm(u_tile(v))
                rank_mm(u_tile(v))
            with pe.If(left < T):
                with pe.Fori(left, T) as u:
                    turn_in(u_tile(u))
                    x1_mm(u_tile(u))
                    turn_y(u_tile(u))
                    gate_mm(u_tile(u))
                    rank_mm(u_tile(u))
            pe.wait_ge(s_wc, 5)
            pe.matmul(bank[6][:, 0:X], ones[:], msum[:], start=True, stop=True).then_inc(s_r_mm, 1)
            pe.wait_ge(s_wc, 6)
            for k in range(2):
                ins = pe.matmul(bank[6][0:1, k * P:(k + 1) * P], tcol[:, k:k + 1], ident[:], start=True, stop=True)
            ins.then_inc(s_r_mm, 1)

            def turn_rows(i, b, n):
                pe.wait_ge(s_e_x[b], n * 16 + 16)
                transpose(bank[b], ys[b], s_e_tp)

            def out_mm(i, b, n):
                pe.wait_ge(s_e_w2[b], n * 32 + 32)
                pe.wait_ge(s_e_hT, i + 1)
                wait_from(pe, s_e_ev, i - 1)
                for f in range(4):
                    ins = pe.matmul(bank[4 + b][:, 0:D], hT[b][:, f, :], we2[b][:, f, :], start=f == 0,
                                    stop=f == 3)
                ins.then_inc(s_e_o, 1)

            def e_tile(i, b, n, last):
                if not last:
                    turn_rows(i + 1, 1 - b, n + b)
                pe.wait_ge(s_e_w1[b], n * 32 + 32)
                pe.wait_ge(s_e_yT, i + 1)
                for f in range(4):
                    for a in range(2):
                        ins = pe.matmul(bank[2 + b][:, f * P:(f + 1) * P], we1[b][:, a, f * P:(f + 1) * P],
                                        yT[b][:, a, :], start=a == 0, stop=a == 1)
                ins.then_inc(s_e_h, 1)
                if not isinstance(i, int) or i > 0:
                    out_mm(i - 1, 1 - b, n + b - 1)

            pe.wait_ge(s_eid, 1)
            half = half_of(pe)
            turn_rows(0, 0, 0)
            in_pairs(pe, half, e_tile)
            out_mm(half * 2, 0, half)

        @block.vector
        def _(dve):
            own = Links(dve, s_dve)
            link = own.link

            marks = iter(range(64))

            def mark(signal):
                c = next(marks)
                dve.memset(scr[:, c:c + 1], 0.0).then_inc(signal, 1)

            def col(a, t):
                return a[:, t:t + 1] if isinstance(t, int) else a[:, bass.ds(t, 1)]

            def deviations(t0, n, ready, rooted, at):
                dve.tensor_scalar(sda[:, t0:t0 + n], mva[:, t0:t0 + n, 1], EPS, None, ALU.add).then_inc(ready, 1)
                dve.wait_ge(rooted, at)
                link(dve.reciprocal(rsa[:, t0:t0 + n], sda[:, t0:t0 + n]))

            dve.wait_ge(s_sch_ld, 16)
            link(dve.tensor_reduce(mnmx[:, :, 0], dgr[:], AX.X, ALU.min))
            link(dve.tensor_reduce(mnmx[:, :, 1], dgr[:], AX.X, ALU.max))
            dve.tensor_scalar(tiles[:], mnmx[:], 7, None, ALU.arith_shift_right).then_inc(s_sch, 1)

            for c in range(NC):
                dve.wait_ge(s_x[c], 16)
                block = range(c * CT, (c + 1) * CT)
                for t in block:
                    own.post(dve.bn_stats(st_b[:, t % CT, :], acc[:, t * D:(t + 1) * D]))
                own.until(0)
                for t in block:
                    own.post(dve.bn_aggr(mva[:, t, :], st_b[:, t % CT, :]))
                own.until(0)
                deviations(c * CT, CT, s_xv, s_xs, c + 1)
                for t in block:
                    a = acc[:, t * D:(t + 1) * D]
                    ins = dve.tensor_scalar(a, a, mva[:, t, 0:1], rsa[:, t:t + 1], ALU.subtract, ALU.mult)
                ins.then_inc(s_xn, 1)

            dve.wait_ge(s_wt, CONST)
            link(dve.tensor_copy(dstf[:], dsti[:]))
            wv = wkv[:].rearrange("p a (h c) -> p (a h) c", c=HD)
            link(dve.tensor_reduce(hsum[:], wv, AX.X, ALU.add))
            link(dve.tensor_scalar(hsum[:], hsum[:], 1.0 / HD, None, ALU.mult))
            link(dve.tensor_tensor(wv, wv, hsum[:].unsqueeze(2).broadcast_to([P, 2 * H2, HD]), ALU.subtract))
            dve.wait_ge(s_w, 1)
            for i in range(2):
                link(dve.tensor_copy(w12[:, i, :], bank[4 + i][:, 0:D]))
            link(dve.memset(one_row[:], 1.0))
            dve.wait_ge(s_sch_ld, 32)
            tb = tab[:].rearrange("o (l g) m -> o l g m", l=2)
            link(dve.tensor_tensor(cnt[:], trow[:, :, 1], trow[:, :, 0], ALU.subtract))
            link(dve.tensor_scalar(cnt[:], cnt[:], 1.0, None, ALU.add))
            link(dve.tensor_tensor_scan(cum[:], one_row[:], cnt[:], 0.0, ALU.mult, ALU.add))
            link(dve.tensor_copy(tb[:, 0, :, 1], cum[:]))
            link(dve.tensor_tensor(tb[:, 0, :, 0], cum[:], cnt[:], ALU.subtract))
            for c in range(2):
                link(dve.tensor_scalar(tb[:, 1, :, c], tb[:, 0, :, c], cum[:, NG - 1:NG], None, ALU.add))
            for l in range(2):
                link(dve.tensor_tensor(tb[:, l, :, 2], trow[:, :, 0], tb[:, l, :, 0], ALU.subtract))
            for l in range(2):
                link(dve.tensor_scalar(tb[:, l, :, 2], tb[:, l, :, 2], float(STEPS), None, ALU.add))
            link(dve.memset(tmin[0][:], float(T)))
            link(dve.memset(tmin[1][:], float(T)))
            link(dve.tensor_reduce(tmin[0][:, 0:T], trow[:, :, 0].rearrange("o (i b) -> o i b", b=GB), AX.X, ALU.min))
            for k in range(6):
                link(dve.tensor_tensor(tmin[(k + 1) % 2][:, 0:T], tmin[k % 2][:, 0:T],
                                       tmin[k % 2][:, 1 << k:T + (1 << k)], ALU.min))
            link(dve.memset(fin[:], 0.0))
            link(dve.tensor_tensor_scan(fin[:, 1:T + 1], one_row[:, 0:T], tmin[0][:, 0:T], 0.0, ALU.add, ALU.min))
            link(dve.tensor_tensor(has[:], fin[:, 1:T + 1], fin[:, 0:T], ALU.subtract))
            link(dve.tensor_scalar(has[:], has[:], -float(T), float(T), ALU.mult, ALU.add))
            link(dve.memset(made_i[:, 0:1], float(T)))
            link(dve.tensor_tensor(made_i[:, 1:T + 1], has[:], fin[:, 0:T], ALU.add))
            link(dve.tensor_copy(made_i[:, T + 1:T + 2], fin[:, T:T + 1]))
            link(dve.tensor_scalar(made_i[:, T + 2:T + 3], fin[:, T:T + 1], -1.0, float(NI), ALU.mult, ALU.add))
            mark(s_tab)
            dve.wait_ge(s_tab, 1)
            link(dve.memset(kvT[:], 0.0))
            link(dve.memset(msum[:], 0.0))
            link(dve.memset(yk[:], 0.0))
            link(dve.memset(pidx[:], float(NO_SLOT)))
            dve.memset(scr[:, 63:64], 0.0).then_inc(s_d_yst, 16)
            dve.wait_ge(s_pool, 6)
            link(dve.tensor_copy(iota_x[:], iota_n[:, 0:X]))
            link(dve.tensor_scalar(eoff[:], iota_x[:], float(REG), None, ALU.mult))
            for k in range(2):
                link(dve.tensor_scalar(plc[:, :, k], tok[:], float(k * NP), None, ALU.add))
            dve.wait_ge(s_xst, 16 * NC)
            link(dve.memset(acc[:], 0.0))
            for k in range(2):
                mark(s_ev)
            for k in range(CG):
                dve.memset(hot[k][:, 0:1], 0.0).then_inc(s_used[k], 1)
            mark(s_wc)
            dve.wait_ge(s_pool, 6)
            dve.wait_ge(s_wc, 1)

            def hot_group(i, b, layer, before):
                g = i * GB + b
                before, after, shift = group_steps(dve, g + NG * layer, before)
                with dve.Fori(before, after) as step:
                    t = tile_of(step, shift)
                    for k in range(CG):
                        c = g * CG + k
                        dve.wait_ge(s_used[k], step + 1)
                        dve.tensor_scalar(hot[k][:], iota_n[:, bass.ds(t * P, P)], dstf[:, bass.ds(c, 1)],
                                          wts[:, bass.ds(c, 1)], ALU.is_equal, ALU.mult).then_inc(s_oh[k], 1)
                return after

            def kv_vars(i):
                dve.wait_ge(s_m_sq, i + 1)
                link(dve.tensor_reduce(r8[:, 0, :], sq[:].rearrange("p (h c) -> p h c", c=HD), AX.X, ALU.add))
                dve.tensor_scalar(r8[:, 0, :], r8[:, 0, :], 1.0 / HD, EPS, ALU.mult, ALU.add).then_inc(s_m_var, 1)

            def kv_norm(i):
                dve.wait_ge(s_m_sd, i + 1)
                link(dve.reciprocal(r8[:, 1, :], r8[:, 1, :]))
                wait_from(dve, s_m_acc, i)
                link(dve.tensor_tensor(kvn[:].rearrange("p (h c) -> p h c", c=HD),
                                       bank[2][:].rearrange("p (h c) -> p h c", c=HD),
                                       r8[:, 1, :].unsqueeze(2).broadcast_to([P, H2, HD]), ALU.mult))
                link(dve.tensor_tensor(kvn[:], kvn[:], kvg[:], ALU.mult))
                dve.tensor_tensor(kvn[:], kvn[:], kvb[:], ALU.add).then_inc(s_m_kvn, 1)

            def edge_turn(i):
                before = None
                for b in range(GB):
                    before = hot_group(i, b, 0, before)
                    if b == 1:
                        kv_vars(i)
                    if b == 2:
                        kv_norm(i)

            edge_turn(0)
            own.enter()
            with dve.Fori(1, NI) as i:
                own.turn(i - 1, 4)
                edge_turn(i)
            own.leave(NI - 1, 4)
            dve.wait_ge(s_m_acc, T)
            for h in range(4):
                p, o = h // 2, (h % 2) * HD
                link(dve.tensor_scalar(kvT[o:o + HD, p, o:o + HD], bank[3][o:o + HD, p * P + o:p * P + o + HD],
                                       1.0 / N, None, ALU.mult))
            mark(s_wc)
            dve.wait_ge(s_w, 2)
            for p in range(2):
                link(dve.tensor_copy(t1[:, p, :], bank[4 + p][:, 0:D]))
            mark(s_wc)
            dve.wait_ge(s_w, 3)
            for p in range(2):
                link(dve.tensor_copy(mixm[:, p, :], bank[6 - 5 * p][:, 0:D]))
            dve.wait_ge(s_h1, 16 * T)
            link(dve.memset(acc[:], 0.0))
            mark(s_wc)

            own_x = Parts(dve, s_dve_x, (3, 1, 12))
            xlink = own_x.link
            own_p = Parts(dve, s_dve_p, (6,))
            plink = own_p.link

            def x1_rows(u):
                own_x.start(u, 0)
                dve.wait_ge(s_d_mm, u + 1)
                dve.wait_ge(s_d_x, u * 16 + 16)
                xlink(dve.tensor_tensor(xs[:], bank[2][:, 0:D], xin[:], ALU.add))
                dve.tensor_tensor(x1s[:], xs[:], bo_s[:], ALU.add).then_inc(s_d_x1, 1)
                dve.wait_ge(s_d_x1, u + 1)
                dve.tensor_tensor(xs[:], x1s[:], bet[:], ALU.add).then_inc(s_d_xb, 1)
                xlink(dve.bn_stats(st6[:], x1s[:]))
                dve.nop(nofuse=True)
                xlink(dve.bn_aggr(mv[:], st6[:]))
                dve.tensor_scalar(rs[:, 0:1], mv[:, 1:2], EPS, None, ALU.add).then_inc(s_d_var, 1)

            def y_rows(u):
                own_x.start(u, 1)
                dve.wait_ge(s_d_sd, u + 1)
                xlink(dve.reciprocal(rs[:, 2:3], rs[:, 1:2]))
                dve.wait_ge(s_d_yst, u * 16 + 16)
                dve.tensor_scalar(yr[:], x1s[:], mv[:, 0:1], rs[:, 2:3], ALU.subtract, ALU.mult).then_inc(s_d_y, 1)

            def choose(u):
                own_x.start(u, 2)
                dve.wait_ge(s_d_lg, u + 1)
                xlink(dve.tensor_tensor(lg[:, 0, :], bank[4][:, 0:X], gb[:], ALU.add))
                for k in range(2):
                    xlink(dve.tensor_reduce(tmx[:, k:k + 1], lg[:, k, :], AX.X, ALU.max))
                    xlink(dve.tensor_scalar(ne[:], lg[:, k, :], tmx[:, k:k + 1], float(X), ALU.not_equal, ALU.mult))
                    xlink(dve.tensor_tensor(ne[:], ne[:], iota_x[:], ALU.add))
                    xlink(dve.tensor_reduce(tix[:, k:k + 1], ne[:], AX.X, ALU.min))
                    xlink(dve.tensor_scalar(ohx[:, k, :], iota_x[:], tix[:, k:k + 1], None, ALU.is_equal))
                    if k == 0:
                        xlink(dve.scalar_tensor_tensor(out=lg[:, 1, :], in0=ohx[:, 0, :], scalar=-3.0e38,
                                                       in1=lg[:, 0, :], op0=ALU.mult, op1=ALU.add))
                dve.tensor_tensor(mask[:], ohx[:, 0, :], ohx[:, 1, :], ALU.add).then_inc(s_r_mask, 1)

            def place(u):
                own_p.start(u, 0)
                plink(dve.tensor_copy(mxa[:, bass.ds(u, 1), :].rearrange("p o k -> p (o k)"), tmx[:]))
                dve.wait_ge(s_d_yk, u + 1)
                dve.wait_ge(s_r_mm, u + 1)
                plink(dve.tensor_tensor(rank[:], bank[5][:, 0:X], eoff[:], ALU.add))
                plink(dve.tensor_tensor(prod[:], ohx[:], rank[:].unsqueeze(1).broadcast_to([P, 2, X]), ALU.mult))
                plink(dve.tensor_reduce(posf[:], prod[:], AX.X, ALU.add))
                plink(dve.tensor_copy(pidx[:], posf[:]))
                plink(dve.tensor_tensor(msum[:], msum[:], mask[:], ALU.add))
                dve.nop(nofuse=True)

            def turn_done():
                dve.memset(scr[:, 62:63], 0.0).then_inc(s_r_turn, 1)

            def x1_turn(i):
                v, u = made(dve, i), made(dve, i + 1)
                before = None
                for b in range(GB):
                    before = hot_group(i, b, 1, before)
                    if b == 1:
                        with dve.If(v < T):
                            choose(u_tile(v))
                    if b == 2:
                        with dve.If(u < T):
                            x1_rows(u_tile(u))
                    if b == 3:
                        wait_from(dve, s_sc, i * 32)
                        dve.memset(pidx[:], float(NO_SLOT)).then_inc(s_r_none, 1)
                        dve.wait_ge(s_r_none, i + 1)
                        dve.nop(nofuse=True)
                        with dve.If(v < T):
                            place(u_tile(v))
                        turn_done()
                        with dve.If(u < T):
                            y_rows(u_tile(u))

            x1_turn(0)
            with dve.Fori(1, NI) as i:
                x1_turn(i)
            v, left, more = made(dve, NI), left_of(dve), later(dve)
            dve.wait_ge(s_sc, 32 * NI)
            link(dve.memset(pidx[:], float(NO_SLOT)))
            with dve.If(v < T):
                choose(u_tile(v))
                place(u_tile(v))
            turn_done()
            with dve.If(left < T):
                with dve.Fori(left, T) as u:
                    x1_rows(u_tile(u))
                    y_rows(u_tile(u))
                    choose(u_tile(u))
                    place(u_tile(u))
                    turn_done()
            dve.wait_ge(s_gdone, GB + 2 * NG)
            mark(s_wc)
            dve.wait_ge(s_r_mm, T + 1)
            link(dve.tensor_copy(rank[:], bank[6][:, 0:X]))
            link(dve.tensor_scalar(nt_i[:], rank[:], float(P - 1), None, ALU.add))
            link(dve.tensor_scalar(nt_i[:], nt_i[:], 7, None, ALU.arith_shift_right))
            link(dve.tensor_copy(nt_f[:, 0, :], nt_i[:]))
            link(dve.tensor_tensor_scan(nt_f[:, 1, :], ones[:, 0:X], nt_f[:, 0, :], 0.0, ALU.mult, ALU.add))
            dve.tensor_tensor(ends[:], rank[0:1, :], eoff[0:1, :], ALU.add).then_inc(s_ends, 1)
            link(dve.tensor_scalar(ne[:], nt_f[:, 1, :], tok[:, 0:1], None, ALU.is_le))
            link(dve.tensor_reduce(tcol[:, 0:1], ne[:], AX.X, ALU.add))
            link(dve.tensor_tensor(ne[:], ne[:], nt_f[:, 0, :], ALU.mult))
            link(dve.tensor_reduce(tcol[:, 1:2], ne[:], AX.X, ALU.add))
            link(dve.tensor_tensor(tcol[:, 1:2], tok[:, 0:1], tcol[:, 1:2], ALU.subtract))
            link(dve.tensor_scalar(tcol[:, 1:2], tcol[:, 1:2], float(P), None, ALU.mult))
            link(dve.tensor_scalar(tcol[:, 2:3], tcol[:, 0:1], float(REG), None, ALU.mult))
            link(dve.tensor_tensor(tcol[:, 1:2], tcol[:, 1:2], tcol[:, 2:3], ALU.add))
            mark(s_wc)
            dve.wait_ge(s_r_mm, T + 2)
            link(dve.tensor_copy(erow[:], bank[6][0:1, P:P + ST]))
            link(dve.tensor_scalar(eraw[:, 0, :], bank[6][0:1, 0:ST], float(X - 1), None, ALU.min))
            link(dve.memset(eraw[:, 1, :], 0.0))
            link(dve.tensor_tensor(eraw[:, 1, 2:ST], eraw[:, 0, 2:ST], eraw[:, 0, 0:ST - 2], ALU.is_equal))
            link(dve.tensor_scalar(eraw[:, 1, :], eraw[:, 1, :], float(X), None, ALU.mult))
            link(dve.tensor_copy(pairs[:], nt_f[0:1, 1, X - 1:X]))
            link(dve.tensor_scalar(pairs[:], pairs[:], 1, None, ALU.arith_shift_right))
            link(dve.tensor_scalar(pairs[:], pairs[:], -1.0, None, ALU.add))
            dve.tensor_tensor(eid[:], eraw[:, 0, :], eraw[:, 1, :], ALU.max).then_inc(s_eid, 1)
            dve.tensor_tensor(pw[1][:], mxa[:, :, 1], mxa[:, :, 0], ALU.subtract).then_inc(s_pd, 1)
            dve.wait_ge(s_exp, 1)
            link(dve.tensor_scalar(pw[0][:], pw[1][:], 1.0, None, ALU.add))
            link(dve.reciprocal(pw[0][:], pw[0][:]))
            link(dve.tensor_tensor(pw[1][:], pw[1][:], pw[0][:], ALU.mult))

            def e_tile(i, b, n, last):
                wait_from(dve, s_e_st[b], n * 16)
                dve.wait_ge(s_e_yT, i + 1)
                dve.tensor_copy(eplc[b][:], places[:, bass.ds(i, 1)])
                dve.wait_ge(s_e_o, i + 1)
                dve.tensor_tensor(eo[b], bank[4 + b][:, 0:D], be2[b], ALU.add).then_inc(s_e_ev, 1)

            dve.wait_ge(s_eid, 1)
            in_pairs(dve, half_of(dve), e_tile)

            def c_tile(i, b, n):
                first = not isinstance(i, int) or i < T
                second = not isinstance(i, int) or i > 0
                p = (b - 1) % FS
                c = cy[b]
                if first:
                    dve.wait_ge(s_f_ld[b], n * 32 + 32)
                    own.post(dve.scalar_tensor_tensor(out=c[0], in0=c[1], scalar=col(pw[0], i), in1=c[0],
                                                      op0=ALU.mult, op1=ALU.add))
                if second:
                    dve.wait_ge(s_f_sd, i)
                    own.post(dve.reciprocal(crs[p][:, 2:3], crs[p][:, 1:2]))
                if first:
                    own.until(1 if second else 0)
                    own.post(dve.scalar_tensor_tensor(out=c[0], in0=c[2], scalar=col(pw[1], i), in1=c[0],
                                                      op0=ALU.mult, op1=ALU.add))
                if second:
                    own.until(1 if first else 0)
                    dve.scalar_tensor_tensor(out=crs[p][:, 3:4], in0=cmv[p][:, 0:1], scalar=-1.0,
                                             in1=crs[p][:, 2:3], op0=ALU.mult, op1=ALU.mult).then_inc(s_f_r, 1)
                if first:
                    own.until(0)
                    link(dve.bn_stats(st6[:], c[0]))
                    dve.nop(nofuse=True)
                    link(dve.bn_aggr(cmv[b][:], st6[:]))
                    dve.tensor_scalar(crs[b][:, 0:1], cmv[b][:, 1:2], EPS, None, ALU.add).then_inc(s_f_var, 1)

            for i in range(FS):
                c_tile(i, i, 0)
            own.enter()
            with dve.Fori(1, T // FS) as j:
                own.turn(j - 1, 5 * FS)
                for b in range(FS):
                    c_tile(j * FS + b, b, j)
            own.leave(T // FS - 1, 5 * FS)
            for i in range(T // FS * FS, T + 1):
                c_tile(i, i % FS, i // FS)


def kernel(**inputs):
    import numpy as np
    import concourse.bacc as bacc
    from concourse.bass_utils import run_bass_kernel_spmd as run

    def pad(a, value):
        return np.concatenate([np.asarray(a), np.full((EP - E,), value, np.asarray(a).dtype)])

    def columns(a):
        return np.ascontiguousarray(a.reshape(NCH, P).T)

    f = {k: np.asarray(v) for k, v in inputs.items()}
    dst = pad(f["dst"], N - 1)
    arrays = {
        "x": np.concatenate([f["x"], np.zeros((NP - N, D), np.float32)]),
        "src_t": columns(pad(f["src"], 0)),
        "dst_t": columns(dst),
        "dst_g": dst.reshape(DG, 2, P * CG),
        "wt_t": columns(pad(f["edge_weight"], 0)),
        "w1t": f["L0_gnn_W1"].T,
        "gw2": f["L0_gnn_W2"],
        "wq": f["L0_mix_wq"],
        "wkv_t": np.concatenate([f["L0_mix_wk"], f["L0_mix_wv"]]).T,
        "wo_t": f["L0_mix_wo"].T,
        "bo": f["L0_mix_bo"],
        "kv_g": np.concatenate([f["L0_mix_ln_k_g"]] * 4 + [f["L0_mix_ln_v_g"]] * 4),
        "kv_b": np.concatenate([f["L0_mix_ln_k_b"]] * 4 + [f["L0_mix_ln_v_b"]] * 4),
        "gate_w": f["L0_ffn_gate_w"],
        "gate_b": f["L0_ffn_gate_b"],
        "w1": f["L0_ffn_w1"],
        "b1_t": f["L0_ffn_b1"].reshape(X, FF // P, P).transpose(0, 2, 1),
        "w2": f["L0_ffn_w2"],
        "b2": f["L0_ffn_b2"],
        "gamma": f["L0_ffn_gamma"],
        "beta": f["L0_ffn_beta"],
    }
    nc = bacc.Bacc("TRN2", target_bir_lowering=False, num_devices=1)
    given, args = {}, []
    for name, a in arrays.items():
        a = np.ascontiguousarray(a)
        given[f"in_{name}"] = a
        args.append(nc.dram_tensor(f"in_{name}", a.shape, mybir.dt.from_np(a.dtype), kind="ExternalInput").ap())
    args.append(nc.dram_tensor("out_rows", (NP, D), F32, kind="ExternalOutput").ap())
    gps_layer(nc, *args)
    r = run(nc, [given], core_ids=[0])
    return r.results[0]["out_rows"][:N]
```
